# Optimizing a Trainium2 kernel written in Bass

```python
import numpy as np
import jax
import jax.numpy as jnp

def _softmax(x, axis=-1):
    return jax.nn.softmax(x, axis=axis)

def _gelu(x):
    return jax.nn.gelu(x, approximate=True)

def _silu(x):
    return jax.nn.silu(x)

def _sigmoid(x):
    return jax.nn.sigmoid(x)

def _layernorm(x, axis=-1, eps=1e-05):
    m = jnp.mean(x, axis=axis, keepdims=True)
    v = jnp.var(x, axis=axis, keepdims=True)
    return (x - m) / jnp.sqrt(v + eps)

def _scatter_add(tgt, idx, src, axis=0):
    return tgt.at[idx].add(src)

def _segment_sum(src, seg, n):
    return jax.ops.segment_sum(src, seg, n)
kernel_name = 'mk_adaln_d1_jaxref_r4_8f7cc7'

def setup_inputs(seed: int=0):
    np.random.seed(seed)
    _w = jnp.asarray

    def _L0_attn_setup():
        import jax, jax.numpy as jnp
        import numpy as np
        import math
        DIM = 256
        H = 16
        DK = DIM // H
        SEG = 128
        NN = 2
        DIL = 4
        B, L = (2, 2048)

        def _attn(q, k, v):
            scores = jnp.einsum('bshqd,bshkd->bshqk', q, k) / math.sqrt(q.shape[-1])
            a = jax.nn.softmax(scores, axis=-1)
            return jnp.einsum('bshqk,bshkd->bshqd', a, v)
        key = jax.random.key(seed)
        ks = jax.random.split(key, 9)
        scale = 1.0 / math.sqrt(DIM)

        def lin(k):
            return jax.random.normal(k, (DIM, DIM), jnp.float32) * scale
        return {'x': jax.random.normal(ks[0], (B, L, DIM), jnp.float32), 'Wq': lin(ks[1]), 'bq': jnp.zeros((DIM,), jnp.float32), 'Wk': lin(ks[2]), 'bk': jnp.zeros((DIM,), jnp.float32), 'Wv': lin(ks[3]), 'bv': jnp.zeros((DIM,), jnp.float32), 'Wo': lin(ks[4]), 'bo': jnp.zeros((DIM,), jnp.float32)}
    _L0_attn_in = _L0_attn_setup()

    def _L0_ffn_setup():
        import jax, jax.numpy as jnp
        import numpy as np
        B, N, D, E, R, K = (4, 512, 256, 8, 64, 2)
        key = jax.random.key(seed)
        ks = jax.random.split(key, 5)
        scale = 0.02
        return {'x': jax.random.normal(ks[0], (B, N, D), dtype=jnp.float32), 'gate_w': jax.random.normal(ks[1], (D, E), dtype=jnp.float32) * scale, 'Wu': jax.random.normal(ks[2], (E, D, R), dtype=jnp.float32) * scale, 'Wv': jax.random.normal(ks[3], (E, D, R), dtype=jnp.float32) * scale, 'Wo': jax.random.normal(ks[4], (E, R, D), dtype=jnp.float32) * scale}
    _L0_ffn_in = _L0_ffn_setup()
    _L0_c = _w((lambda *s: np.random.randn(*s).astype(np.float32) * 0.05)(8, 256))
    _L0_wmod = _w((lambda *s: np.random.randn(*s).astype(np.float32) * 0.05)(256, 6 * 256) * 256 ** (-0.5))
    _d = {'L0_attn_x': _L0_attn_in['x'], 'L0_attn_Wq': _L0_attn_in['Wq'], 'L0_attn_bq': _L0_attn_in['bq'], 'L0_attn_Wk': _L0_attn_in['Wk'], 'L0_attn_bk': _L0_attn_in['bk'], 'L0_attn_Wv': _L0_attn_in['Wv'], 'L0_attn_bv': _L0_attn_in['bv'], 'L0_attn_Wo': _L0_attn_in['Wo'], 'L0_attn_bo': _L0_attn_in['bo'], 'L0_ffn_gate_w': _L0_ffn_in['gate_w'], 'L0_ffn_Wu': _L0_ffn_in['Wu'], 'L0_ffn_Wv': _L0_ffn_in['Wv'], 'L0_ffn_Wo': _L0_ffn_in['Wo'], 'L0_c': _L0_c, 'L0_wmod': _L0_wmod}
    _x0 = _d['L0_attn_x']
    _d['L0_attn_x'] = jax.random.normal(jax.random.fold_in(jax.random.key(seed), 1), (8, 2048, 256), dtype=_x0.dtype)
    del _x0
    return _d

def reference(L0_attn_x, L0_attn_Wq, L0_attn_bq, L0_attn_Wk, L0_attn_bk, L0_attn_Wv, L0_attn_bv, L0_attn_Wo, L0_attn_bo, L0_ffn_gate_w, L0_ffn_Wu, L0_ffn_Wv, L0_ffn_Wo, L0_c, L0_wmod):

    def _L0_attn_ref(x, Wq, bq, Wk, bk, Wv, bv, Wo, bo):
        import jax, jax.numpy as jnp
        import numpy as np
        import math
        DIM = 256
        H = 16
        DK = DIM // H
        SEG = 128
        NN = 2
        DIL = 4
        B, L = (2, 2048)

        def _attn(q, k, v):
            scores = jnp.einsum('bshqd,bshkd->bshqk', q, k) / math.sqrt(q.shape[-1])
            a = jax.nn.softmax(scores, axis=-1)
            return jnp.einsum('bshqk,bshkd->bshqd', a, v)
        Bx, Lx, C = x.shape
        pad = -Lx % SEG

        def proj_chunk(W, b):
            t = x @ W + b
            t = jnp.pad(t, ((0, 0), (0, pad), (0, 0)))
            S = t.shape[1] // SEG
            t = t.reshape(Bx, S, SEG, H, DK)
            return t.transpose(0, 1, 3, 2, 4)
        q = proj_chunk(Wq, bq)
        k = proj_chunk(Wk, bk)
        v = proj_chunk(Wv, bv)
        S = q.shape[1]
        out = _attn(q, k, v)
        dil_idx = jnp.arange(0, SEG, DIL)
        kd = k[:, :, :, dil_idx, :]
        vd = v[:, :, :, dil_idx, :]
        seg_ids = jnp.arange(S)
        w = 1.0 / (2 * NN)
        for off in range(1, NN + 1):
            for sign in (-1, 1):
                n = seg_ids + sign * off
                valid = (n >= 0) & (n < S)
                nc = jnp.clip(n, 0, S - 1)
                cross = _attn(q, kd[:, nc], vd[:, nc])
                out = out + jnp.where(valid[None, :, None, None, None], cross * w, 0.0)
        out = out.transpose(0, 1, 3, 2, 4).reshape(Bx, S * SEG, C)
        out = out[:, :Lx, :]
        return out @ Wo + bo

    def _L0_ffn_ref(x, gate_w, Wu, Wv, Wo):
        import jax, jax.numpy as jnp
        import numpy as np
        B, N, D, E, R, K = (4, 512, 256, 8, 64, 2)
        logits = jnp.einsum('bnd,de->bne', x, gate_w)
        topv, topi = jax.lax.top_k(logits, K)
        w = jax.nn.softmax(topv, axis=-1)
        u = jnp.einsum('bnd,edr->bner', x, Wu)
        v = jnp.einsum('bnd,edr->bner', x, Wv)
        s = jax.nn.silu(u) * v
        Y = jnp.einsum('bner,erd->bned', s, Wo)
        y_sel = jnp.take_along_axis(Y, topi[..., None], axis=2)
        out = jnp.einsum('bnkd,bnk->bnd', y_sel, w)
        return out
    x = L0_attn_x
    mod = (_silu(L0_c) @ L0_wmod).reshape(L0_c.shape[0], 6, 1, -1)
    sa, ca, ga, sb, cb, gb = (mod[:, 0], mod[:, 1], mod[:, 2], mod[:, 3], mod[:, 4], mod[:, 5])
    ga = (2 * (ga >= 0) - 1) * jnp.maximum(jnp.abs(ga), 0.25)
    gb = (2 * (gb >= 0) - 1) * jnp.maximum(jnp.abs(gb), 0.25)
    h = _layernorm(x, axis=-1) * (1 + ca) + sa
    x = x + ga * _L0_attn_ref(h, L0_attn_Wq, L0_attn_bq, L0_attn_Wk, L0_attn_bk, L0_attn_Wv, L0_attn_bv, L0_attn_Wo, L0_attn_bo)
    h = _layernorm(x, axis=-1) * (1 + cb) + sb
    x = x + gb * _L0_ffn_ref(h, L0_ffn_gate_w, L0_ffn_Wu, L0_ffn_Wv, L0_ffn_Wo)
    return x

_drawn_inputs = setup_inputs


def setup_inputs(seed=0):
    import zlib

    import numpy as np

    out = dict(_drawn_inputs(seed))
    spreads = {'L0_attn_bq': (0.0, 0.8),
     'L0_attn_bk': (0.0, 0.8),
     'L0_attn_bv': (0.0, 0.1),
     'L0_attn_bo': (0.0, 0.332)}
    factors = {'L0_ffn_gate_w': 8.0, 'L0_ffn_Wu': 8.0, 'L0_ffn_Wv': 8.0, 'L0_ffn_Wo': 8.0}
    for name, (base, spread) in spreads.items():
        noise = np.random.default_rng([zlib.crc32(name.encode()), seed]).standard_normal(out[name].shape)
        drawn = base * np.exp(spread * noise) if base else spread * noise
        out[name] = jnp.asarray(drawn.astype(out[name].dtype))
    for name, factor in factors.items():
        out[name] = (out[name] * factor).astype(out[name].dtype)
    return out
```

```python
from contextlib import ExitStack

import concourse.bass as bass
from concourse import mybir

ALU = mybir.AluOpType
ACT = mybir.ActivationFunctionType
AX_X = mybir.AxisListType.X
F32 = mybir.dt.float32
F32R = mybir.dt.float32r
BF16 = mybir.dt.bfloat16
U32 = mybir.dt.uint32

P = 128
DIM = 256
CH = DIM // P
HEADS = 16
DK = DIM // HEADS
HP = HEADS // CH
DIL = 4
ND = P // DIL
NG = 5
NEXP, RANK = 8, 64
ER = NEXP * RANK
EPS = 1e-5
SLOTS = 12
STACK = 6 * DK
ROWS = STACK + 2 * SLOTS
Q_PARTS = [0, 0, 1, 0, 2, 1]
K_PARTS = [0, 1, 0, 2, 0, 1]
VW = DK + 1
RING = 4
PROBS = 4
CONST_LOADS = 32
SILU_READY = 1
GATES_READY = 15
SETUP_V = 42
ONEHOT_READY = 7
SETUP_P = 10


def view(ap, dims):
    return bass.AP(ap.tensor, ap.offset, [ap.ap[0]] + [list(d) for d in dims])


def wait(eng, sem, value):
    if not (isinstance(value, int) and value <= 0):
        eng.wait_ge(sem, value)


def wait_apart(eng, sem, value, passed):
    if not (isinstance(value, int) and value <= 0):
        eng.wait_ge(sem, value)
        eng.sem_inc(passed, 1)


def adaln_block(nc, x, wq, bq, wk, bk, wv, bv, wo, bo, gate_w, w_up, w_gate, w_down, c, wmod, out):
    batches, length, _ = x.shape
    segs = length // P
    pairs = batches * segs // 2
    seq_pairs = segs // 2
    seq_shift = seq_pairs.bit_length() - 1
    assert seq_pairs == 1 << seq_shift and pairs % RING == 0 and 2 * RING == 8

    x_pairs = x.rearrange("b (s i p) d -> (b s) p i d", i=2, p=P)
    out_pairs = out.rearrange("b (s i p) d -> (b s) p i d", i=2, p=P)

    ctx = ExitStack()
    with ctx:
        def sb(name, shape, dt=F32):
            return ctx.enter_context(nc.sbuf_tensor(name, shape, dt))

        def sem(name):
            return ctx.enter_context(nc.semaphore(name))

        part_scr = nc.dram_tensor("part_scr", [RING, 2, P, 3, CH * 2 * P], BF16, kind="Internal").ap()
        vseg_words = ND * HEADS * VW
        v_scr = nc.dram_tensor("v_scr", [batches * (segs + 4), ND, HEADS * VW], F32, kind="Internal").ap()
        m_scr = nc.dram_tensor("m_scr", [RING, 2, NG, HEADS, 2, P], BF16, kind="Internal").ap()
        g_scr = nc.dram_tensor("g_scr", [batches, 3 * DIM], F32, kind="Internal").ap()

        ident = sb("ident", [P, P])
        iota8 = sb("iota8", [P, NEXP])
        neg_half = sb("neg_half", [P, 2])
        w_hi = sb("w_hi", [P, 5120], F32R)
        w_lo = sb("w_lo", [P, 5120], F32R)
        gatew = sb("gatew", [P, CH, NEXP])
        bqk = sb("bqk", [P, 2, CH])
        bv_bc = sb("bv_bc", [P, DIM])
        modT = sb("modT", [P, 4 * CH * batches + 1])
        onehot = sb("onehot", [P, SLOTS], F32)
        cT = sb("cT", [P, CH, batches])
        sT_c = sb("sT_c", [P, CH, batches])
        gates8 = sb("gates8", [batches, 3 * DIM])
        gtmp = sb("gtmp", [batches, 2, 2 * DIM])
        bo8 = sb("bo8", [batches, DIM])

        QS = sb("QS", [P, RING, HP, CH, 2 * P], BF16)
        KS = sb("KS", [P, RING, HP, CH, 2 * P], BF16)
        KD = sb("KD", [P, HP * CH, SLOTS, ND], BF16)
        v_own = sb("v_own", [P, RING, 2, HEADS, VW])
        v_dil = sb("v_dil", [P, 2, HEADS * VW])
        v_blk = sb("v_blk", [P, 2, HEADS, 4, VW])
        probs = sb("probs", [P, PROBS, CH, 2, P])
        mx = sb("mx", [P, 2, HP, CH, 8])
        negm = sb("negm", [P, NG, HEADS])
        mparts = sb("mparts", [P, 2, NG, HEADS], BF16)
        identb = sb("identb", [P, P], BF16)
        mT = sb("mT", [P, 2, P], BF16)
        rsum = sb("rsum", [P, 2, 4 * NG])
        o_grp = sb("o_grp", [P, HEADS, NG, DK])
        o_half = sb("o_half", [P, HEADS, 2, DK])
        o_sum = sb("o_sum", [P, 2, HEADS, DK])

        x_in = sb("x_in", [P, 2, 2, DIM])
        x_res = sb("x_res", [P, 2, 2, DIM])
        gates = sb("gates", [P, 2, 3 * DIM])
        st1 = sb("st1", [P, 2, 6])
        mv1 = sb("mv1", [P, 2, 2])
        ve1 = sb("ve1", [P, 2])
        rs1 = sb("rs1", [P, 2])
        st2 = sb("st2", [P, 2, 6])
        mv2 = sb("mv2", [P, 2, 2])
        ve2 = sb("ve2", [P, 2])
        rs2 = sb("rs2", [P, 2])
        h32 = sb("h32", [P, CH, 2 * P])
        h_hi = sb("h_hi", [P, CH, 2 * P], F32R)
        h_lo = sb("h_lo", [P, CH, 2 * P], F32R)
        qk32 = sb("qk32", [P, 2, CH, 2 * P])
        parts = sb("parts", [P, 2, 3, CH * 2 * P], BF16)
        o32 = sb("o32", [P, CH, 2 * P])
        oT_hi = sb("oT_hi", [P, CH, 2 * P], F32R)
        oT_lo = sb("oT_lo", [P, CH, 2 * P], F32R)
        xn2 = sb("xn2", [P, 2, DIM])
        g32 = sb("g32", [P, CH, 2 * P])
        g_hi = sb("g_hi", [P, CH, 2 * P], F32R)
        g_lo = sb("g_lo", [P, CH, 2 * P], F32R)
        logits = sb("logits", [P, 2, NEXP])
        top = sb("top", [P, 2, NEXP])
        topi = sb("topi", [P, 2, NEXP], U32)
        topf = sb("topf", [P, 2, 2])
        dlt = sb("dlt", [P, 2])
        ed = sb("ed", [P, 2])
        den = sb("den", [P, 2])
        wsel = sb("wsel", [P, 2, 2])
        wone = sb("wone", [P, 2, 2, NEXP])
        wexp = sb("wexp", [P, 2, NEXP])
        th = sb("th", [P, ER])
        s_act = sb("s_act", [P, 2, ER])
        y32 = sb("y32", [P, DIM])
        s32 = sb("s32", [P, 4, P])
        sT_hi = sb("sT_hi", [P, 4, P], F32R)
        sT_lo = sb("sT_lo", [P, 4, P], F32R)

        stage = view(KS[:, 0, 0, 0, 0:2 * P].bitcast(F32), [(1, 8192)])

        ps_m = [ctx.enter_context(nc.psum_tensor(f"ps_m{n}", [P, 512], F32)) for n in range(2)]
        ps_s = [ctx.enter_context(nc.psum_tensor(f"ps_s{n}", [P, 512], F32)) for n in range(2)]
        ps_o = [ctx.enter_context(nc.psum_tensor(f"ps_o{n}", [P, 512], F32)) for n in range(2)]
        ps_d = [ctx.enter_context(nc.psum_tensor(f"ps_d{n}", [P, 512], F32)) for n in range(2)]

        const_in = sem("const_in")
        gates_out = sem("gates_out")
        pads_out = sem("pads_out")
        w_ready = sem("w_ready")
        setup_v = sem("setup_v")
        setup_p = sem("setup_p")
        setup_a = sem("setup_a")
        setup_t = sem("setup_t")
        x_loaded = sem("x_loaded")
        res_loaded = sem("res_loaded")
        part_out = [sem("qpart_out"), sem("kpart_out")]
        stack_in = [sem("q_stacked"), sem("k_stacked")]
        v_out = sem("v_out")
        vdil_in = [sem("vdil_in0"), sem("vdil_in1")]
        m_out = sem("m_out")
        m_in = [sem("m_in0"), sem("m_in1")]
        stored = sem("stored")
        xT_done = sem("xT_done")
        qkv_done = sem("qkv_done")
        mT_done = sem("mT_done")
        oT_done = sem("oT_done")
        attn_done = sem("attn_done")
        gT_done = sem("gT_done")
        lg_done = sem("lg_done")
        uv_done = sem("uv_done")
        sT_done = sem("sT_done")
        down_done = sem("down_done")
        sm_done = sem("sm_done")
        ss_done = sem("ss_done")
        av_done = sem("av_done")
        ln1_done = sem("ln1_done")
        ln1_var = sem("ln1_var")
        rs1_done = sem("rs1_done")
        h_evac = sem("h_evac")
        h_split = sem("h_split")
        qk_evac = sem("qk_evac")
        qk_split = sem("qk_split")
        v_evac = sem("v_evac")
        kd_done = sem("kd_done")
        max_done = sem("max_done")
        mp_done = sem("mp_done")
        mT_evac = sem("mT_evac")
        exp_done = sem("exp_done")
        vblk_done = sem("vblk_done")
        norm_done = sem("norm_done")
        osum_done = sem("osum_done")
        oT_evac = sem("oT_evac")
        oT_split = sem("oT_split")
        attn_evac = sem("attn_evac")
        xb_done = sem("xb_done")
        ln2_var = sem("ln2_var")
        rs2_done = sem("rs2_done")
        ln2_done = sem("ln2_done")
        g_evac = sem("g_evac")
        g_split = sem("g_split")
        lg_read = sem("lg_read")
        dlt_done = sem("dlt_done")
        ed_done = sem("ed_done")
        w_done = sem("w_done")
        th_done = sem("th_done")
        s1_done = sem("s1_done")
        s2_done = sem("s2_done")
        s3_done = sem("s3_done")
        sT_evac = sem("sT_evac")
        sT_split = sem("sT_split")
        y_done = sem("y_done")
        res_done = sem("res_done")
        x1_done = sem("x1_done")
        own_ln1 = sem("own_ln1")
        own_ln2 = sem("own_ln2")
        own_mp = sem("own_mp")
        own_nm = sem("own_nm")
        own_tt = sem("own_tt")
        own_qk = sem("own_qk")
        own_os = sem("own_os")
        settled = sem("settled")



        block = ctx.enter_context(nc.Block())

        def on(pair):
            return not isinstance(pair, int) or 0 <= pair < pairs

        def done(pair):
            return min(max(pair + 1, 0), pairs) if isinstance(pair, int) else pair + 1

        def rows_of(t, pair):
            if isinstance(pair, int):
                return t[pair]
            return t[bass.ds(pair, 1)].rearrange("a p i d -> (a p) i d")

        def run_steps(eng, step):
            for p in range(-4, RING):
                step(p, p % RING)
            with eng.Fori(1, pairs // RING - 1) as it:
                for u in range(RING):
                    step(RING * it + u, u)
            for p in range(pairs - RING, pairs + 2):
                step(p, p % RING)

        def seq_of(pair):
            return pair >> seq_shift

        def v_slot(pair):
            return (pair + 2 * seq_of(pair)) * 2 + 2

        @block.sync
        def _(sp):
            loads = 0

            def const_load(dst, src):
                sp.dma_start(dst, src).then_inc(const_in, 16)
                return 1

            def staged(at, n):
                return stage[:, at:at + n]

            loads += const_load(staged(5120, 3072).rearrange("p (k n) -> p k n", k=CH),
                                wmod.rearrange("(k p) n -> p k n", p=P))
            with nc.allow_non_contiguous_dma(reason="small constants, once"):
                for k in range(CH):
                    loads += const_load(cT[:, k, :], c[:, k * P:(k + 1) * P].rearrange("b p -> p b"))
                loads += const_load(bqk[:, 0, :], bq.rearrange("(k p) -> p k", p=P))
                loads += const_load(bqk[:, 1, :], bk.rearrange("(k p) -> p k", p=P))
            loads += const_load(bo8[:, :], bass.AP(bo.tensor, 0, [[0, batches], [1, DIM]]))
            loads += const_load(bv_bc[:, :], bass.AP(bv.tensor, 0, [[0, P], [1, DIM]]))
            loads += const_load(gatew[:, :, :], gate_w.rearrange("(k p) e -> p k e", p=P))
            for n, w in enumerate((wq, wk, wv)):
                loads += const_load(staged(512 * n, 512).rearrange("p (k n) -> p k n", k=CH),
                                    w.rearrange("(k p) n -> p k n", p=P))
            for j in range(HP):
                for k in range(CH):
                    row = (2 * j + k) % HP * DK
                    loads += const_load(stage[row:row + DK, 1536 + (j // 4) * DIM:1536 + (j // 4 + 1) * DIM],
                                        wo[(k * HP + j) * DK:(k * HP + j + 1) * DK, :])
            for n, w in enumerate((w_up, w_gate)):
                for k in range(CH):
                    loads += const_load(
                        staged(2048 + 1024 * n + 512 * k, 512).rearrange("p (e r) -> p e r", e=NEXP),
                        w[:, k * P:(k + 1) * P, :].rearrange("e p r -> p e r"))
            loads += const_load(staged(4096, 1024).rearrange("p (k n) -> p k n", k=4),
                                w_down.rearrange("e r n -> (e r) n").rearrange("(k p) n -> p k n", p=P))
            assert loads == CONST_LOADS
            sp.wait_ge(setup_v, GATES_READY)
            sp.dma_start(g_scr, gates8[:, :]).then_inc(gates_out, 16)
            sp.wait_ge(setup_p, 1)
            for b in range(batches):
                for e in (0, segs + 2):
                    at = b * (segs + 4) + e
                    sp.dma_start(v_scr[at:at + 2, :, :].rearrange("s j w -> (s j) w"),
                                 v_blk[0:2 * ND, 0, 0:4, :, :].rearrange("p a g w -> p (a g w)"),
                                 ).then_inc(pads_out, 16)
            sp.wait_ge(gates_out, 16)
            sp.wait_ge(pads_out, 32 * batches)

            def maxima(pair, u, i):
                wait_apart(sp, mT_evac, 2 * pair + i + 1, settled)
                sp.dma_start(m_scr[u, i].rearrange("g h a q -> (g h) a q"), mT[0:NG * HEADS, :, :]).then_inc(m_out, 16)
                wait_apart(sp, m_out, 16 * (2 * pair + i + 1), settled)
                wait_apart(sp, m_in[i], 32 * pair, settled)
                for a in range(2):
                    row = STACK + a * SLOTS + 2 * u + i
                    sp.dma_start(QS[row:row + NG, u, :, :, i * P:(i + 1) * P].rearrange("g j k q -> g (j k) q"),
                                 m_scr[u, i, :, :, a, :]).then_inc(m_in[i], 16)

            def stacks(pair, u, n):
                wait_apart(sp, part_out[n], 16 * (pair + 1), settled)
                wait_apart(sp, ss_done, 16 * (pair - RING + 1), settled)
                wait_apart(sp, stack_in[n], 96 * pair, settled)
                dst = (QS, KS)[n]
                for blk, part in enumerate((Q_PARTS, K_PARTS)[n]):
                    row = 3 * CH * 2 * P
                    src = bass.AP(part_scr.tensor, part_scr[u, n, 0, part, 0:1].offset,
                                  [[row, DK], [DK * row, HP], [1, CH * 2 * P]])
                    sp.dma_start(dst[blk * DK:(blk + 1) * DK, u, :, :, :].rearrange("c j k t -> c j (k t)"),
                                 src).then_inc(stack_in[n], 16)

            def step(p, u):
                if on(p + 4):
                    wait_apart(sp, x_loaded, 16 * (p + 4), settled)
                    wait_apart(sp, xT_done, p + 3, settled)
                    sp.dma_start(x_in[:, u % 2, :, :], rows_of(x_pairs, p + 4)).then_inc(x_loaded, 16)
                if on(p - 1):
                    wait_apart(sp, res_loaded, 32 * (p - 1), settled)
                    wait_apart(sp, stored, 16 * (p - 2), settled)
                    sp.dma_start(x_res[:, (u + 1) % 2, :, :], rows_of(x_pairs, p - 1)).then_inc(res_loaded, 16)
                    sp.dma_start(gates[:, (u + 1) % 2, :],
                                 bass.AP(g_scr.tensor, seq_of(p - 1) * (3 * DIM), [[0, P], [1, 3 * DIM]])
                                 ).then_inc(res_loaded, 16)
                if on(p):
                    wait_apart(sp, v_out, 16 * done(p + 1), settled)
                    wait_apart(sp, vblk_done, 2 * p, settled)
                    sp.dma_start(v_dil[:, 1, :], neighbours(v_slot(p) + 1)).then_inc(vdil_in[1], 16)
                    maxima(p, u, 1)
                if on(p - 2):
                    wait_apart(sp, res_done, 2 * (p - 1), settled)
                    sp.dma_start(rows_of(out_pairs, p - 2), x_res[:, u % 2, :, :]).then_inc(stored, 16)
                a = (u + 3) % RING
                if on(p + 3):
                    for n in range(2):
                        wait_apart(sp, qk_split, 2 * (p + 3) + n + 1, settled)
                        sp.dma_start(part_scr[a, n].rearrange("p s t -> p (s t)"),
                                     parts[:, n, :, :].rearrange("p s t -> p (s t)")).then_inc(part_out[n], 16)
                    wait_apart(sp, v_out, 16 * (p + 3), settled)
                    wait_apart(sp, v_evac, p + 4, settled)
                    at = v_slot(p + 3)
                    sp.dma_start(
                        bass.AP(v_scr.tensor, at * vseg_words, [[HEADS * VW, ND], [vseg_words, 2], [1, HEADS * VW]]),
                        v_own[0:P:DIL, a, :, :, :].rearrange("p i h w -> p i (h w)")).then_inc(v_out, 16)
                    stacks(p + 3, a, 0)
                if on(p + 1):
                    wait_apart(sp, v_out, 16 * done(p + 2), settled)
                    wait_apart(sp, vblk_done, 2 * p + 1, settled)
                    sp.dma_start(v_dil[:, 0, :], neighbours(v_slot(p + 1))).then_inc(vdil_in[0], 16)
                    maxima(p + 1, (u + 1) % RING, 0)
                if on(p + 3):
                    stacks(p + 3, a, 1)

            def neighbours(slot):
                return bass.AP(v_scr.tensor, (slot - 2) * vseg_words,
                               [[3 * vseg_words, 2], [HEADS * VW, 2 * ND], [1, HEADS * VW]])

            run_steps(sp, step)
            sp.wait_ge(stored, 16 * pairs)
            sp.wait_ge(v_out, 16 * pairs)
            sp.wait_ge(m_out, 32 * pairs)
            for n in range(2):
                sp.wait_ge(part_out[n], 16 * pairs)

        @block.tensor
        def _(pe):
            def split_mm(dst, stat, mov, first, last):
                (s_hi, s_lo), (m_hi, m_lo) = stat, mov
                nc.tensor.matmul(dst, s_hi, m_hi, start=first, stop=False)
                nc.tensor.matmul(dst, s_hi, m_lo, start=False, stop=False)
                return nc.tensor.matmul(dst, s_lo, m_hi, start=False, stop=last)

            def w(at, n):
                return w_hi[:, at:at + n], w_lo[:, at:at + n]

            pe.wait_ge(setup_a, 2)
            pe.wait_ge(const_in, 16 * CONST_LOADS)
            mods = stage[:, 5120:8192].rearrange("p (k n) -> p k n", k=CH)
            for n, m in enumerate((1, 0, 4, 3)):
                for k in range(CH):
                    at = (n * CH + k) * batches
                    for kk in range(CH):
                        col = m * DIM + k * P
                        nc.tensor.matmul(ps_d[0][:, at:at + batches], mods[:, kk, col:col + P], sT_c[:, kk, :],
                                         start=(kk == 0), stop=(kk == CH - 1))
            for n, m in enumerate((2, 5)):
                for kk in range(CH):
                    mm = nc.tensor.matmul(ps_d[1][0:batches, n * DIM:(n + 1) * DIM], sT_c[:, kk, :],
                                          mods[:, kk, m * DIM:(m + 1) * DIM], start=(kk == 0), stop=(kk == CH - 1))
            mm.then_inc(setup_t, 1)
            pe.wait_ge(setup_v, SETUP_V)
            pe.wait_ge(setup_p, SETUP_P)

            def x_transposed(p, u):
                pe.wait_ge(ln1_done, p + 1)
                if on(p - 5):
                    pe.wait_ge(s2_done, 2 * done(p - 5))
                else:
                    wait(pe, v_evac, done(p - 1))
                    wait(pe, mT_evac, 2 * done(p - 3) - 1)
                for k in range(CH):
                    for i in range(2):
                        mm = nc.tensor.transpose(ps_d[0][:, (2 * k + i) * P:(2 * k + i + 1) * P],
                                                 x_in[:, u % 2, i, k * P:(k + 1) * P], ident[:, :])
                mm.then_inc(xT_done, 1)

            def down(p, i):
                pe.wait_ge(sT_split, 2 * p + i + 1)
                if i == 1:
                    pe.wait_ge(qk_evac, 2 * done(p + 5))
                for e in range(4):
                    mm = split_mm(ps_d[1][:, 0:DIM], (sT_hi[:, e, :], sT_lo[:, e, :]),
                                  w(4096 + e * DIM, DIM), e == 0, e == 3)
                mm.then_inc(down_done, 1)

            def maxima_transposed(p, i):
                pe.wait_ge(mp_done, 2 * p + i + 1)
                for a in range(2):
                    mm = nc.tensor.transpose(ps_d[0][0:NG * HEADS, a * 64:(a + 1) * 64].bitcast(BF16),
                                             mparts[:, a, :, :].rearrange("p g h -> p (g h)"), identb[:, :])
                mm.then_inc(mT_done, 1)

            def experts_transposed(p, i):
                pe.wait_ge(s3_done, 2 * p + i + 1)
                for e in range(4):
                    mm = nc.tensor.transpose(ps_d[1][:, e * P:(e + 1) * P], s_act[:, i, e * P:(e + 1) * P],
                                             ident[:, :])
                mm.then_inc(sT_done, 1)

            def project(p, n):
                pe.wait_ge(h_split, p + 1)
                for k in range(CH):
                    for kk in range(CH):
                        mm = split_mm(ps_d[n][:, k * 2 * P:(k + 1) * 2 * P],
                                      w(512 * n + kk * DIM + k * P, P),
                                      (h_hi[:, kk, :], h_lo[:, kk, :]), kk == 0, kk == CH - 1)
                mm.then_inc(qkv_done, 1)

            def project_v(p):
                pe.wait_ge(qk_evac, 2 * p + 1)
                for i in range(2):
                    for kk in range(CH):
                        mm = split_mm(ps_d[0][:, i * DIM:(i + 1) * DIM],
                                      (h_hi[:, kk, i * P:(i + 1) * P], h_lo[:, kk, i * P:(i + 1) * P]),
                                      w(1024 + kk * DIM, DIM), kk == 0, kk == CH - 1)
                mm.then_inc(qkv_done, 1)

            def o_transposed(p):
                pe.wait_ge(osum_done, 2 * p + 2)
                pe.wait_ge(v_evac, done(p + 4))
                pe.wait_ge(mT_evac, 2 * done(p + 1))
                for k in range(CH):
                    for i in range(2):
                        mm = nc.tensor.transpose(
                            ps_d[0][:, (2 * k + i) * P:(2 * k + i + 1) * P],
                            o_sum[:, i, k * HP:(k + 1) * HP, :].rearrange("p h c -> p (h c)"), ident[:, :])
                mm.then_inc(oT_done, 1)

            def project_out(p):
                pe.wait_ge(oT_split, p + 1)
                wait(pe, y_done, 2 * p)
                if not on(p - 1):
                    pe.wait_ge(qk_evac, 2 * done(p + 4))
                for i in range(2):
                    for kk in range(CH):
                        mm = split_mm(ps_d[1][:, i * DIM:(i + 1) * DIM],
                                      (oT_hi[:, kk, i * P:(i + 1) * P], oT_lo[:, kk, i * P:(i + 1) * P]),
                                      w(1536 + kk * DIM, DIM), kk == 0, kk == CH - 1)
                mm.then_inc(attn_done, 1)

            def g_transposed(p):
                pe.wait_ge(ln2_done, p + 1)
                for k in range(CH):
                    for i in range(2):
                        mm = nc.tensor.transpose(ps_d[1][:, (2 * k + i) * P:(2 * k + i + 1) * P],
                                                 xn2[:, i, k * P:(k + 1) * P], ident[:, :])
                mm.then_inc(gT_done, 1)

            def gate_logits(p):
                pe.wait_ge(g_evac, p + 1)
                pe.wait_ge(mT_evac, min(2 * p + 5, 2 * pairs) if isinstance(p, int) else 2 * p + 5)
                for i in range(2):
                    for kk in range(CH):
                        mm = nc.tensor.matmul(ps_d[0][:, i * NEXP:(i + 1) * NEXP], g32[:, kk, i * P:(i + 1) * P],
                                              gatew[:, kk, :], start=(kk == 0), stop=(kk == CH - 1))
                mm.then_inc(lg_done, 1)

            def experts_up(p, i):
                pe.wait_ge(g_split, p + 1)
                for n in range(2):
                    if n == 0 and i == 1:
                        pe.wait_ge(s1_done, 2 * p + 1)
                    if n == 1:
                        pe.wait_ge(lg_read, p + 1)
                        if i == 1:
                            pe.wait_ge(s2_done, 2 * p + 1)
                    for kk in range(CH):
                        mm = split_mm(ps_d[1 - n][:, :],
                                      (g_hi[:, kk, i * P:(i + 1) * P], g_lo[:, kk, i * P:(i + 1) * P]),
                                      w(2048 + 1024 * n + 512 * kk, ER), kk == 0, kk == CH - 1)
                    mm.then_inc(uv_done, 1)

            def near_keys(rows, j, k, r):
                return view(KD[0:rows, 2 * j + k, r, 0:1], [(3 * ND, 2), (1, 2 * ND)])

            def scores_for_max(p, u, t):
                i, j = divmod(t, HP)
                if t == 0:
                    pe.wait_ge(stack_in[0], 96 * (p + 1))
                    pe.wait_ge(stack_in[1], 96 * (p + 1))
                    pe.wait_ge(kd_done, done(p + 1))
                wait(pe, max_done, 16 * p + t - 1)
                bank = ps_m[t % 2]
                own = slice(i * P, (i + 1) * P)
                for k in range(CH):
                    q = QS[0:STACK, u, j, k, own]
                    nc.tensor.matmul(bank[:, 2 * k * P:(2 * k + 1) * P], q, KS[0:STACK, u, j, k, own],
                                     start=True, stop=True)
                    mm = nc.tensor.matmul(bank[:, (2 * k + 1) * P:(2 * k + 2) * P], q,
                                          near_keys(STACK, j, k, 2 * u + i), start=True, stop=True)
                mm.then_inc(sm_done, 1)

            def scores_for_exp(p, u, t):
                i, j = divmod(t, HP)
                if j == 0:
                    pe.wait_ge(m_in[i], 32 * (p + 1))
                wait(pe, exp_done, 16 * p + t - 1)
                bank = ps_s[t % 2]
                own = slice(i * P, (i + 1) * P)
                for k in range(CH):
                    q = QS[0:ROWS, u, j, k, own]
                    nc.tensor.matmul(bank[:, 2 * k * P:(2 * k + 1) * P], KS[0:ROWS, u, j, k, own], q,
                                     start=True, stop=True)
                    for half in range(2):
                        slot = 2 * u + i + 3 * half
                        mm = nc.tensor.matmul(
                            bank[half * 2 * ND:(half + 1) * 2 * ND, (2 * k + 1) * P:(2 * k + 2) * P],
                            KD[0:ROWS, 2 * j + k, slot:slot + 2, :].rearrange("p s n -> p (s n)"), q,
                            start=True, stop=True)
                mm.then_inc(ss_done, 1)

            def probs_times_v(p, u, t):
                i, j = divmod(t, HP)
                pe.wait_ge(exp_done, 16 * p + t + 1)
                if t == 0:
                    pe.wait_ge(v_evac, p + 1)
                if j == 0:
                    pe.wait_ge(vblk_done, 2 * p + i + 1)
                if t % 2 == 0:
                    wait(pe, norm_done, 8 * p + t // 2 - 1)
                bank = ps_o[t // 2 % 2]
                for k in range(CH):
                    at = (2 * (t % 2) + k) * NG * VW
                    pr = probs[:, t % PROBS, k, :, :]
                    nc.tensor.matmul(bank[:, at:at + 4 * VW], pr[:, 1, :],
                                     v_blk[:, i, k * HP + j, :, :].rearrange("p g w -> p (g w)"),
                                     start=True, stop=True)
                    mm = nc.tensor.matmul(bank[:, at + 4 * VW:at + NG * VW], pr[:, 0, :],
                                          v_own[:, u, i, k * HP + j, :], start=True, stop=True)
                mm.then_inc(av_done, 1)

            def step(p, u):
                for t in range(16):
                    if t == 0 and on(p + 3):
                        x_transposed(p + 3, (u + 3) % RING)
                    if t == 0 and on(p - 2):
                        down(p - 2, 0)
                    if t == 1 and on(p):
                        pe.wait_ge(h_evac, done(p + 3))
                        wait(pe, s2_done, 2 * done(p - 2))
                        maxima_transposed(p, 1)
                    if t == 1 and on(p - 2):
                        pe.wait_ge(y_done, 2 * (p - 2) + 1)
                        experts_transposed(p - 2, 1)
                    if t == 2 and on(p + 3):
                        wait(pe, mT_evac, 2 * done(p))
                        project(p + 3, 0)
                    if t == 3 and on(p + 3):
                        wait(pe, sT_evac, 2 * done(p - 2))
                        wait(pe, qk_evac, 2 * done(p + 2))
                        project(p + 3, 1)
                    if t == 4 and on(p + 3):
                        project_v(p + 3)
                    if t == 4 and on(p - 2):
                        down(p - 2, 1)
                    if t == 5 and on(p - 1):
                        o_transposed(p - 1)
                    if t == 6 and on(p - 1):
                        project_out(p - 1)
                    if t == 9 and on(p + 1):
                        wait(pe, oT_evac, done(p - 1))
                        pe.wait_ge(v_evac, done(p + 3))
                        maxima_transposed(p + 1, 0)
                    if t == 9 and on(p - 1):
                        g_transposed(p - 1)
                    if t == 10 and on(p - 1):
                        gate_logits(p - 1)
                    if t == 11 and on(p - 1):
                        experts_up(p - 1, 0)
                    if t == 13 and on(p - 1):
                        experts_up(p - 1, 1)
                    if t == 15 and on(p - 1):
                        pe.wait_ge(s1_done, 2 * p)
                        experts_transposed(p - 1, 0)
                    if on(p):
                        scores_for_exp(p, u, t)
                    if on(p + 1):
                        scores_for_max(p + 1, (u + 1) % RING, t)
                    if t >= 2 and on(p):
                        probs_times_v(p, u, t - 2)
                    if t < 2 and on(p - 1):
                        probs_times_v(p - 1, (u + 3) % RING, t + 14)

            run_steps(pe, step)

        @block.scalar
        def _(act):
            act.wait_ge(const_in, 16 * CONST_LOADS)
            nc.scalar.activation(sT_c[:, :, :], cT[:, :, :], ACT.Tanh, scale=0.5).then_inc(setup_a, 1)
            act.wait_ge(setup_v, SILU_READY)
            nc.scalar.activation(sT_c[:, :, :], sT_c[:, :, :], ACT.Copy, scale=0.5).then_inc(setup_a, 1)
            act.wait_ge(setup_v, SETUP_V)

            def mod(n, k, pair):
                return modT[:, bass.ds((n * CH + k) * batches + seq_of(pair), 1)]

            def modulated(p, bank, n, full, high):
                for dst in (full, high):
                    for k in range(CH):
                        ins = nc.scalar.activation(dst[:, k, :], ps_d[bank][:, k * 2 * P:(k + 1) * 2 * P],
                                                   ACT.Identity, scale=mod(n, k, p), bias=mod(n + 1, k, p))
                return ins

            def near_copy(p, u):
                act.wait_ge(stack_in[1], 96 * (p + 1))
                wait(act, ss_done, 16 * (p - 2))
                for dup in range(2):
                    slot = (2 * u + 2) % 8 + 8 * dup
                    if slot >= SLOTS:
                        continue
                    src = view(KS[0:STACK, u, 0, 0, 0:1], [(2 * P, HEADS), (P, 2), (DIL, ND)])
                    ins = nc.scalar.activation(KD[0:STACK, :, slot:slot + 2, :], src, ACT.Copy)
                ins.then_inc(kd_done, 1)

            def v_blocks(p, i):
                act.wait_ge(vdil_in[i], 16 * (p + 1))
                wait(act, av_done, 16 * (p - 1) + 8 * i + 8)
                for g in range(4):
                    rows = slice(g * ND, (g + 1) * ND)
                    ins = nc.scalar.activation(
                        v_blk[rows, i, :, g, 0:DK],
                        v_dil[rows, i, :].rearrange("p (h w) -> p h w", h=HEADS)[:, :, 0:DK], ACT.Copy)
                ins.then_inc(vblk_done, 1)

            def exps(p, t):
                act.wait_ge(ss_done, 16 * p + t + 1)
                wait(act, av_done, 16 * p + t - PROBS + 1)
                nc.scalar.activation(probs[:, t % PROBS, :, :, :].rearrange("p k n q -> p (k n q)"),
                                     ps_s[t % 2][:, :], ACT.Exp).then_inc(exp_done, 1)

            def max_evac(p, i):
                act.wait_ge(mT_done, 2 * p + i + 1)
                wait(act, m_out, 16 * (2 * p + i))
                nc.scalar.activation(mT[0:NG * HEADS, :, :].rearrange("p a q -> p (a q)"),
                                     ps_d[0][0:NG * HEADS, 0:P].bitcast(BF16), ACT.Copy).then_inc(mT_evac, 1)

            def qk_copy(p, n):
                act.wait_ge(qkv_done, 3 * p + n + 1)
                wait(act, qk_split, 2 * (p - 1) + n + 1)
                wait(act, part_out[n], 16 * p)
                scale = (0.25, 1.0)[n]
                for k in range(CH):
                    src = ps_d[n][:, k * 2 * P:(k + 1) * 2 * P]
                    nc.scalar.activation(qk32[:, n, k, :], src, ACT.Identity, scale=scale, bias=bqk[:, n, k:k + 1])
                    ins = nc.scalar.activation(parts[:, n, 0, k * 2 * P:(k + 1) * 2 * P], src, ACT.Identity,
                                               scale=scale, bias=bqk[:, n, k:k + 1])
                ins.then_inc(qk_evac, 1)

            def s_copy(p, i):
                act.wait_ge(sT_done, 2 * p + i + 1)
                wait(act, down_done, 2 * p + i)
                wait(act, sT_split, 2 * p + i)
                src = ps_d[1][:, :]
                nc.scalar.activation(s32[:, :, :].rearrange("p e t -> p (e t)"), src, ACT.Copy)
                nc.scalar.activation(sT_hi[:, :, :].rearrange("p e t -> p (e t)"), src, ACT.Copy).then_inc(sT_evac, 1)

            def tanh_u(p, i):
                act.wait_ge(uv_done, 4 * p + 2 * i + 1)
                wait(act, s1_done, 2 * p + i)
                nc.scalar.activation(th[:, :], ps_d[1][:, :], ACT.Tanh, scale=0.5).then_inc(th_done, 1)

            def step(p, u):
                for t in range(16):
                    if t == 0 and on(p + 2):
                        near_copy(p + 2, (u + 2) % RING)
                    if t == 0 and on(p + 3):
                        act.wait_ge(xT_done, p + 4)
                        wait(act, qkv_done, 3 * (p + 3))
                        modulated(p + 3, 0, 0, h32, h_hi).then_inc(h_evac, 1)
                    if t == 1 and on(p):
                        max_evac(p, 1)
                    if t == 1 and on(p - 2):
                        s_copy(p - 2, 1)
                    if t == 2 and on(p + 3):
                        qk_copy(p + 3, 0)
                    if t == 3 and on(p + 3):
                        qk_copy(p + 3, 1)
                    if t == 5 and on(p - 1):
                        act.wait_ge(oT_done, p)
                        wait(act, attn_done, p - 1)
                        src = ps_d[0][:, :]
                        nc.scalar.activation(o32[:, :, :].rearrange("p k t -> p (k t)"), src, ACT.Copy)
                        nc.scalar.activation(oT_hi[:, :, :].rearrange("p k t -> p (k t)"), src,
                                             ACT.Copy).then_inc(oT_evac, 1)
                    if t == 9 and on(p + 1):
                        max_evac(p + 1, 0)
                    if t == 9 and on(p - 1):
                        act.wait_ge(gT_done, p)
                        wait(act, uv_done, 4 * (p - 1))
                        modulated(p - 1, 1, 2, g32, g_hi).then_inc(g_evac, 1)
                    if t == 11 and on(p - 1):
                        act.wait_ge(dlt_done, p)
                        nc.scalar.activation(ed[:, :], dlt[:, :], ACT.Exp).then_inc(ed_done, 1)
                        tanh_u(p - 1, 0)
                    if t == 13 and on(p - 1):
                        tanh_u(p - 1, 1)
                    if on(p):
                        exps(p, t)
                    if t == 5 and on(p):
                        v_blocks(p, 1)
                    if t == 12 and on(p + 1):
                        v_blocks(p + 1, 0)
                    if t == 15 and on(p - 1):
                        s_copy(p - 1, 0)

            run_steps(act, step)

        @block.vector
        def _(dve):
            setup = [0]

            def setup_inc(ins):
                ins.then_inc(setup_v, 1)
                setup[0] += 1
                dve.wait_ge(setup_v, setup[0])

            dve.wait_ge(setup_a, 1)
            setup_inc(nc.vector.scalar_tensor_tensor(out=sT_c[:, :, :], in0=sT_c[:, :, :], scalar=1.0,
                                                     in1=cT[:, :, :], op0=ALU.add, op1=ALU.mult))
            assert setup[0] == SILU_READY
            setup_inc(nc.vector.tensor_copy(w_hi[:, :], stage[:, 0:5120]))
            setup_inc(nc.vector.tensor_tensor(w_lo[:, :], stage[:, 0:5120], w_hi[:, :].bitcast(F32), ALU.subtract))
            setup_inc(nc.vector.tensor_scalar(bqk[:, 0, :], bqk[:, 0, :], 0.25, None, ALU.mult))
            dve.wait_ge(setup_t, 1)
            half = CH * batches
            for n in range(4):
                setup_inc(nc.vector.tensor_scalar(modT[:, n * half:(n + 1) * half],
                                                  ps_d[0][:, n * half:(n + 1) * half],
                                                  1.0 if n % 2 == 0 else 0.0, None, ALU.add))
            raw = gates8[:, 0:2 * DIM]
            setup_inc(nc.vector.tensor_copy(raw, ps_d[1][0:batches, :]))
            setup_inc(nc.vector.tensor_scalar(gtmp[:, 0, :], raw, 0.25, None, ALU.max))
            setup_inc(nc.vector.scalar_tensor_tensor(out=gtmp[:, 0, :], in0=raw, scalar=0.0, in1=gtmp[:, 0, :],
                                                     op0=ALU.is_ge, op1=ALU.mult))
            setup_inc(nc.vector.tensor_scalar(gtmp[:, 1, :], raw, -0.25, None, ALU.min))
            setup_inc(nc.vector.scalar_tensor_tensor(out=gtmp[:, 1, :], in0=raw, scalar=0.0, in1=gtmp[:, 1, :],
                                                     op0=ALU.is_lt, op1=ALU.mult))
            setup_inc(nc.vector.tensor_tensor(raw, gtmp[:, 0, :], gtmp[:, 1, :], ALU.add))
            setup_inc(nc.vector.tensor_tensor(gates8[:, 2 * DIM:3 * DIM], gates8[:, 0:DIM], bo8[:, :], ALU.mult))
            assert setup[0] == GATES_READY
            dve.wait_ge(setup_p, ONEHOT_READY)
            setup_inc(nc.vector.memset(view(QS[:, 0, 0, 0, 0:2 * P].bitcast(U32), [(1, 8192)]), 0))
            setup_inc(nc.vector.memset(view(KD[:, 0, 0, 0:2].bitcast(U32), [(1, HEADS * SLOTS * ND // 2)]), 0))
            for u in range(RING):
                for i in range(2):
                    slot = 2 * u + i + 2
                    setup_inc(nc.vector.tensor_scalar(
                        view(KS[STACK:P, u, 0, 0, i * P:i * P + 1], [(2 * P, HEADS), (1, P)]),
                        view(QS[STACK:P, u, 0, 0, i * P:i * P + 1], [(2 * P, HEADS), (1, P)]),
                        onehot[STACK:P, slot:slot + 1], None, ALU.add))
            for slot in range(SLOTS):
                setup_inc(nc.vector.tensor_scalar(KD[STACK:P, :, slot, :],
                                                  view(QS[STACK:P, 0, 0, 0, 0:1], [(2 * P, HEADS), (1, ND)]),
                                                  onehot[STACK:P, slot:slot + 1], None, ALU.add))
            setup_inc(nc.vector.memset(v_own[:, :, :, :, DK:VW], 1.0))
            dve.wait_ge(pads_out, 32 * batches)
            for g in range(4):
                setup_inc(nc.vector.memset(v_blk[g * ND:(g + 1) * ND, :, :, g, DK:VW], 4.0))
            assert setup[0] == SETUP_V, setup[0]

            def layer_norm_stats(src, st, mv, ve, free_sem, free_val, own, at, done):
                for i in range(2):
                    nc.vector.bn_stats(st[:, i, :], src(i)).then_inc(own, 1)
                wait_apart(dve, own, at + 2, settled)
                for i in range(2):
                    nc.vector.bn_aggr(mv[:, i, :], st[:, i, :]).then_inc(own, 1)
                dve.wait_ge(own, at + 4)
                wait(dve, free_sem, free_val)
                nc.vector.tensor_scalar(ve[:, :], mv[:, :, 1], EPS, None, ALU.add).then_inc(done, 1)

            def norm1_stats(p, u):
                dve.wait_ge(x_loaded, 16 * (p + 1))
                layer_norm_stats(lambda i: x_in[:, u % 2, i, :], st1, mv1, ve1, rs1_done, p, own_ln1, 4 * p, ln1_var)

            def norm1(p, u):
                dve.wait_ge(rs1_done, p + 1)
                for i in range(2):
                    ins = nc.vector.tensor_scalar(x_in[:, u % 2, i, :], x_in[:, u % 2, i, :], mv1[:, i, 0:1],
                                                  rs1[:, i:i + 1], ALU.subtract, ALU.mult)
                ins.then_inc(ln1_done, 1)

            def max_parts(p, i):
                dve.wait_ge(max_done, 16 * p + 8 * i + 8)
                wait(dve, mT_done, 2 * p + i)
                m = view(mx[:, i, 0, 0, 0:1], [(8, HEADS), (1, 8)])
                nc.vector.tensor_reduce(negm[:, 2, :], m[:, :, 0:4], AX_X, ALU.max, negate=True)
                for g, at in ((0, 4), (3, 6)):
                    ins = nc.vector.tensor_scalar(negm[:, g:g + 2, :].rearrange("p g h -> p h g"),
                                                  m[:, :, at:at + 2], -1.0, None, ALU.mult)
                ins.then_inc(own_mp, 1)
                dve.wait_ge(own_mp, 2 * (2 * p + i) + 1)
                flat = negm[:, :, :].rearrange("p g h -> p (g h)")
                nc.vector.tensor_copy(mparts[:, 0, :, :].rearrange("p g h -> p (g h)"), flat).then_inc(own_mp, 1)
                dve.wait_ge(own_mp, 2 * (2 * p + i) + 2)
                nc.vector.tensor_tensor(mparts[:, 1, :, :].rearrange("p g h -> p (g h)"), flat,
                                        mparts[:, 0, :, :].rearrange("p g h -> p (g h)"),
                                        ALU.subtract).then_inc(mp_done, 1)

            def maxima(p, t):
                i, j = divmod(t, HP)
                dve.wait_ge(sm_done, 16 * p + t + 1)
                if j == 0:
                    wait(dve, mp_done, 2 * p + i - 1)
                nc.vector.tensor_reduce(mx[:, i, j, :, :].rearrange("p k s -> p (k s)"),
                                        ps_m[t % 2][:, :].rearrange("p (s n) -> p s n", n=ND),
                                        AX_X, ALU.max).then_inc(max_done, 1)

            def normalise(p, n):
                dve.wait_ge(av_done, 16 * p + 2 * n + 2)
                i, jj = divmod(n, 4)
                if jj == 0:
                    wait(dve, osum_done, 2 * p + i)
                bank = ps_o[n % 2]
                r = rsum[:, n % 2, :]
                nc.vector.reciprocal(r, view(bank[:, DK:DK + 1], [(VW, 4 * NG)])).then_inc(own_nm, 1)
                dve.wait_ge(own_nm, 8 * p + n + 1)
                nc.vector.tensor_tensor(o_grp[:, 4 * jj:4 * jj + 4, :, :].rearrange("p h g c -> p (h g) c"),
                                        view(bank[:, 0:1], [(VW, 4 * NG), (1, DK)]),
                                        view(r, [(1, 4 * NG), (0, DK)]), ALU.mult).then_inc(norm_done, 1)

            def v_copy(p, u):
                dve.wait_ge(qkv_done, 3 * p + 3)
                wait(dve, av_done, 16 * (p - 3))
                for i in range(2):
                    ins = nc.vector.tensor_tensor(v_own[:, u, i, :, 0:DK],
                                                  ps_d[0][:, i * DIM:(i + 1) * DIM].rearrange("p (h c) -> p h c", h=HEADS),
                                                  bv_bc[:, :].rearrange("p (h c) -> p h c", h=HEADS), ALU.add)
                ins.then_inc(v_evac, 1)

            def attn_out(p, u):
                dve.wait_ge(attn_done, p + 1)
                wait(dve, gT_done, p)
                g = gates[:, u % 2, 0:DIM]
                nc.vector.tensor_tensor(xn2[:, :, :], ps_d[1][:, :].rearrange("p (i d) -> p i d", i=2),
                                        view(g, [(0, 2), (1, DIM)]), ALU.mult).then_inc(attn_evac, 1)
                dve.wait_ge(attn_evac, p + 1)
                dve.wait_ge(xb_done, p + 1)
                nc.vector.tensor_tensor(x_res[:, u % 2, :, :], x_res[:, u % 2, :, :], xn2[:, :, :],
                                        ALU.add).then_inc(x1_done, 1)
                dve.wait_ge(x1_done, p + 1)
                layer_norm_stats(lambda i: x_res[:, u % 2, i, :], st2, mv2, ve2, rs2_done, p, own_ln2, 4 * p, ln2_var)

            def norm2(p, u):
                dve.wait_ge(rs2_done, p + 1)
                for i in range(2):
                    ins = nc.vector.tensor_scalar(xn2[:, i, :], x_res[:, u % 2, i, :], mv2[:, i, 0:1],
                                                  rs2[:, i:i + 1], ALU.subtract, ALU.mult)
                ins.then_inc(ln2_done, 1)

            def top_two(p):
                dve.wait_ge(lg_done, p + 1)
                nc.vector.tensor_copy(logits[:, :, :].rearrange("p i e -> p (i e)"),
                                      ps_d[0][:, 0:2 * NEXP]).then_inc(lg_read, 1)
                wait_apart(dve, lg_read, p + 1, settled)
                for i in range(2):
                    nc.vector.max(top[:, i, :], logits[:, i, :]).then_inc(own_tt, 1)
                dve.wait_ge(own_tt, 9 * p + 2)
                nc.vector.tensor_tensor(dlt[:, :], top[:, :, 1], top[:, :, 0], ALU.subtract).then_inc(dlt_done, 1)
                for i in range(2):
                    nc.vector.max_index(topi[:, i, :], top[:, i, :], logits[:, i, :]).then_inc(own_tt, 1)
                dve.wait_ge(own_tt, 9 * p + 4)
                nc.vector.tensor_copy(topf[:, :, :], topi[:, :, 0:2]).then_inc(own_tt, 1)

            def expert_weights(p):
                dve.wait_ge(ed_done, p + 1)
                nc.vector.tensor_scalar(den[:, :], ed[:, :], 2.0, 2.0, ALU.mult, ALU.add).then_inc(own_tt, 1)
                dve.wait_ge(own_tt, 9 * p + 6)
                nc.vector.reciprocal(wsel[:, 0, :], den[:, :]).then_inc(own_tt, 1)
                dve.wait_ge(own_tt, 9 * p + 7)
                nc.vector.tensor_tensor(wsel[:, 1, :], wsel[:, 0, :], ed[:, :], ALU.mult).then_inc(own_tt, 1)
                dve.wait_ge(own_tt, 9 * p + 8)
                for i in range(2):
                    for n in range(2):
                        ins = nc.vector.tensor_scalar(wone[:, n, i, :], iota8[:, :], topf[:, i, n:n + 1],
                                                      wsel[:, n, i:i + 1], ALU.is_equal, ALU.mult)
                ins.then_inc(own_tt, 1)
                dve.wait_ge(own_tt, 9 * p + 9)
                wait(dve, s3_done, 2 * p)
                nc.vector.tensor_tensor(wexp[:, :, :], wone[:, 0, :, :], wone[:, 1, :, :], ALU.add).then_inc(w_done, 1)

            def gated(p, i):
                dve.wait_ge(th_done, 2 * p + i + 1)
                wait(dve, sT_done, 2 * (p - 1) + i + 1)
                nc.vector.scalar_tensor_tensor(out=s_act[:, i, :], in0=th[:, :], scalar=1.0, in1=ps_d[1][:, :],
                                               op0=ALU.add, op1=ALU.mult).then_inc(s1_done, 1)
                dve.wait_ge(s1_done, 2 * p + i + 1)
                dve.wait_ge(uv_done, 4 * p + 2 * i + 2)
                nc.vector.tensor_tensor(s_act[:, i, :], s_act[:, i, :], ps_d[0][:, :], ALU.mult).then_inc(s2_done, 1)

            def experts_out(p, u, i):
                dve.wait_ge(down_done, 2 * p + i + 1)
                wait(dve, res_done, 2 * p + i)
                nc.vector.tensor_tensor(y32[:, :], ps_d[1][:, 0:DIM], gates[:, u % 2, DIM:2 * DIM],
                                        ALU.mult).then_inc(y_done, 1)

            def step(p, u):
                for t in range(16):
                    if t == 0 and on(p):
                        max_parts(p, 1)
                    if t == 0 and on(p - 2):
                        experts_out(p - 2, u, 0)
                    if t == 1 and on(p - 1):
                        normalise(p - 1, 7)
                    if t == 4 and on(p + 3):
                        v_copy(p + 3, (u + 3) % RING)
                    if t == 4 and on(p - 2):
                        experts_out(p - 2, u, 1)
                    if t == 6 and on(p - 1):
                        attn_out(p - 1, u + 1)
                    if t == 8 and on(p + 1):
                        max_parts(p + 1, 0)
                    if t == 8 and on(p - 1):
                        norm2(p - 1, u + 1)
                    if t == 10 and on(p + 4):
                        norm1_stats(p + 4, u)
                    if t == 12 and on(p + 4):
                        norm1(p + 4, u)
                    if t == 10 and on(p - 1):
                        top_two(p - 1)
                    if t == 12 and on(p - 1):
                        expert_weights(p - 1)
                        gated(p - 1, 0)
                    if t == 14 and on(p - 1):
                        gated(p - 1, 1)
                    if on(p + 1):
                        maxima(p + 1, t)
                    if t >= 3 and t % 2 and on(p):
                        normalise(p, (t - 3) // 2)

            run_steps(dve, step)

        @block.gpsimd
        def _(pool):
            nc.gpsimd.memset(v_blk[:, :, :, :, :], 0.0).then_inc(setup_p, 1)
            nc.gpsimd.memset(onehot[:, :], 0.0).then_inc(setup_p, 1)
            nc.gpsimd.memset(ident[:, :], 0.0).then_inc(setup_p, 1)
            nc.gpsimd.memset(identb[:, :], 0.0).then_inc(setup_p, 1)
            nc.gpsimd.memset(neg_half[:, :], -0.5).then_inc(setup_p, 1)
            pool.wait_ge(setup_p, 5)
            count = 5
            for a in range(2):
                nc.gpsimd.affine_select(out=onehot[STACK:P, :], in_=onehot[STACK:P, :], compare_op=ALU.not_equal,
                                        fill=1.0, base=-a * SLOTS, pattern=[[-1, SLOTS]],
                                        channel_multiplier=1).then_inc(setup_p, 1)
                count += 1
                pool.wait_ge(setup_p, count)
            assert count == ONEHOT_READY
            for m in (ident, identb):
                nc.gpsimd.affine_select(out=m[:, :], in_=m[:, :], compare_op=ALU.not_equal, fill=1.0, base=0,
                                        pattern=[[-1, P]], channel_multiplier=1).then_inc(setup_p, 1)
            nc.gpsimd.iota(iota8[:, :], pattern=[[1, NEXP]], base=0, channel_multiplier=0,
                           allow_small_or_imprecise_dtypes=True).then_inc(setup_p, 1)

            pool.wait_ge(setup_p, SETUP_P)

            def low_part(dst, full, high, done):
                nc.gpsimd.tensor_tensor(dst, full, high.bitcast(F32), ALU.subtract).then_inc(done, 1)

            def qk_parts(p, n):
                pool.wait_ge(qk_evac, 2 * p + n + 1)
                x32 = qk32[:, n, :, :].rearrange("p k t -> p (k t)")
                high, mid, low = (parts[:, n, s, :] for s in range(3))
                at = 2 * (2 * p + n)
                nc.gpsimd.tensor_tensor(x32, x32, high, ALU.subtract).then_inc(own_qk, 1)
                wait_apart(pool, own_qk, at + 1, settled)
                nc.gpsimd.tensor_scalar(mid, x32, 1.0, 0.0, ALU.mult, ALU.add).then_inc(own_qk, 1)
                pool.wait_ge(own_qk, at + 2)
                nc.gpsimd.tensor_tensor(low, x32, mid, ALU.subtract).then_inc(qk_split, 1)



            def sum_groups(p, i):
                pool.wait_ge(norm_done, 8 * p + 4 * i + 4)
                wait(pool, oT_done, p)
                at = 2 * (2 * p + i)
                o = o_grp
                nc.gpsimd.tensor_tensor(o_half[:, :, :, :], o[:, :, 0:2, :], o[:, :, 2:4, :],
                                        ALU.add).then_inc(own_os, 1)
                pool.wait_ge(own_os, at + 1)
                nc.gpsimd.tensor_tensor(o_sum[:, i, :, :], o_half[:, :, 0, :], o_half[:, :, 1, :],
                                        ALU.add).then_inc(own_os, 1)
                pool.wait_ge(own_os, at + 2)
                nc.gpsimd.tensor_tensor(o_sum[:, i, :, :], o_sum[:, i, :, :], o[:, :, 4, :],
                                        ALU.add).then_inc(osum_done, 1)

            def flat(t):
                return t[:, :, :].rearrange("p k t -> p (k t)")

            def expert_weight(p, i):
                pool.wait_ge(s2_done, 2 * p + i + 1)
                pool.wait_ge(w_done, p + 1)
                nc.gpsimd.tensor_tensor(s_act[:, i, :].rearrange("p (e r) -> p e r", e=NEXP),
                                        s_act[:, i, :].rearrange("p (e r) -> p e r", e=NEXP),
                                        view(wexp[:, i, 0:1], [(1, NEXP), (0, RANK)]),
                                        ALU.mult).then_inc(s3_done, 1)

            def s_low(p, i):
                pool.wait_ge(sT_evac, 2 * p + i + 1)
                wait(pool, down_done, 2 * p + i)
                low_part(flat(sT_lo), flat(s32), flat(sT_hi), sT_split)

            def last_sum(p, u, i):
                pool.wait_ge(y_done, 2 * p + i + 1)
                nc.gpsimd.tensor_tensor(x_res[:, u % 2, i, :], x_res[:, u % 2, i, :], y32[:, :],
                                        ALU.add).then_inc(res_done, 1)

            def inv_std(ve, rs, var, p, done):
                pool.wait_ge(var, p + 1)
                nc.gpsimd.tensor_tensor(rs[:, :], ve[:, :], neg_half[:, :], ALU.pow).then_inc(done, 1)

            def step(p, u):
                for t in range(16):
                    if t == 0 and on(p - 2):
                        s_low(p - 2, 0)
                        last_sum(p - 2, u, 0)
                    if t == 1 and on(p + 3):
                        pool.wait_ge(h_evac, p + 4)
                        wait(pool, qkv_done, 3 * (p + 3))
                        low_part(flat(h_lo), flat(h32), flat(h_hi), h_split)
                    if t == 1 and on(p - 2):
                        s_low(p - 2, 1)
                    if t == 2 and on(p - 1):
                        sum_groups(p - 1, 1)
                    if t == 2 and on(p + 3):
                        qk_parts(p + 3, 0)
                    if t == 3 and on(p + 3):
                        qk_parts(p + 3, 1)
                    if t == 4 and on(p - 2):
                        last_sum(p - 2, u, 1)

                    if t == 4 and on(p - 1):
                        pool.wait_ge(res_loaded, 32 * p)
                        r = (u + 1) % 2
                        nc.gpsimd.tensor_tensor(x_res[:, r, :, :], x_res[:, r, :, :],
                                                view(gates[:, r, 2 * DIM:2 * DIM + 1], [(0, 2), (1, DIM)]),
                                                ALU.add).then_inc(xb_done, 1)
                    if t == 5 and on(p - 1):
                        pool.wait_ge(oT_evac, p)
                        wait(pool, attn_done, p - 1)
                        low_part(flat(oT_lo), flat(o32), flat(oT_hi), oT_split)
                    if t == 7 and on(p - 1):
                        inv_std(ve2, rs2, ln2_var, p - 1, rs2_done)
                    if t == 10 and on(p):
                        sum_groups(p, 0)
                    if t == 9 and on(p - 1):
                        pool.wait_ge(g_evac, p)
                        wait(pool, uv_done, 4 * (p - 1))
                        low_part(flat(g_lo), flat(g32), flat(g_hi), g_split)
                    if t == 11 and on(p + 4):
                        inv_std(ve1, rs1, ln1_var, p + 4, rs1_done)
                    if t == 13 and on(p - 1):
                        expert_weight(p - 1, 0)
                    if t == 15 and on(p - 1):
                        expert_weight(p - 1, 1)

            run_steps(pool, step)



_INS = ["L0_attn_x", "L0_attn_Wq", "L0_attn_bq", "L0_attn_Wk", "L0_attn_bk", "L0_attn_Wv", "L0_attn_bv",
        "L0_attn_Wo", "L0_attn_bo", "L0_ffn_gate_w", "L0_ffn_Wu", "L0_ffn_Wv", "L0_ffn_Wo", "L0_c", "L0_wmod"]
_OUTS = [((8, 2048, 256), "float32")]


def kernel(**inputs):
    import numpy as _np
    import concourse.bacc as _bacc
    from concourse import mybir as _mybir
    from concourse.bass_utils import run_bass_kernel_spmd as _run

    nc = _bacc.Bacc("TRN2", target_bir_lowering=False, num_devices=1, dynamic_dma_scratch_size=1024)
    arrays, args = {}, []
    for name in _INS:
        a = _np.ascontiguousarray(inputs[name])
        arrays[f"in_{name}_dram"] = a
        args.append(nc.dram_tensor(f"in_{name}_dram", a.shape, _mybir.dt.from_np(a.dtype), kind="ExternalInput").ap())
    for i, (shape, dtype) in enumerate(_OUTS):
        dt = _mybir.dt.from_np(_np.dtype(dtype))
        args.append(nc.dram_tensor(f"out_{i}_dram", shape, dt, kind="ExternalOutput").ap())
    adaln_block(nc, *args)
    r = _run(nc, [arrays], core_ids=[0])
    got = tuple(r.results[0][f"out_{i}_dram"] for i in range(len(_OUTS)))
    return got[0]
```

```python
from contextlib import ExitStack

import concourse.bass as bass
from concourse import mybir

ALU = mybir.AluOpType
ACT = mybir.ActivationFunctionType
AX_X = mybir.AxisListType.X
F32 = mybir.dt.float32
F32R = mybir.dt.float32r
BF16 = mybir.dt.bfloat16
U32 = mybir.dt.uint32

P = 128
DIM = 256
CH = DIM // P
HEADS = 16
DK = DIM // HEADS
HP = HEADS // CH
DIL = 4
ND = P // DIL
NG = 5
NEXP, RANK = 8, 64
ER = NEXP * RANK
EPS = 1e-5
SLOTS = 12
STACK = 6 * DK
ROWS = STACK + 2 * SLOTS
Q_PARTS = [0, 0, 1, 0, 2, 1]
K_PARTS = [0, 1, 0, 2, 0, 1]
VW = DK + 1
HC = 32
OW = 4 * VW + HC
RING = 4
PROBS = 4
MOD_LOADS = 3
CONST_LOADS = 29
SILU_READY = 3
GATES_READY = 14
WEIGHTS_READY = 17
SETUP_V = 27
SETUP_A = 16
ONEHOT_READY = 7
SETUP_P = 12


def view(ap, dims):
    return bass.AP(ap.tensor, ap.offset, [ap.ap[0]] + [list(d) for d in dims])


def wait(eng, sem, value):
    if not (isinstance(value, int) and value <= 0):
        eng.wait_ge(sem, value)


def wait_apart(eng, sem, value, passed):
    if not (isinstance(value, int) and value <= 0):
        eng.wait_ge(sem, value)
        eng.sem_inc(passed, 1)


def adaln_block(nc, x, wq, bq, wk, bk, wv, bv, wo, bo, gate_w, w_up, w_gate, w_down, c, wmod, out):
    batches, length, _ = x.shape
    segs = length // P
    pairs = batches * segs // 2
    seq_pairs = segs // 2
    seq_shift = seq_pairs.bit_length() - 1
    assert seq_pairs == 1 << seq_shift and pairs % RING == 0 and 2 * RING == 8

    x_pairs = x.rearrange("b (s i p) d -> (b s) p i d", i=2, p=P)
    out_pairs = out.rearrange("b (s i p) d -> (b s) p i d", i=2, p=P)

    ctx = ExitStack()
    with ctx:
        def sb(name, shape, dt=F32):
            return ctx.enter_context(nc.sbuf_tensor(name, shape, dt))

        def sem(name):
            return ctx.enter_context(nc.semaphore(name))

        part_scr = nc.dram_tensor("part_scr", [RING, 2, P, 3, CH * 2 * P], BF16, kind="Internal").ap()
        vseg_words = ND * HEADS * VW
        v_scr = nc.dram_tensor("v_scr", [batches * (segs + 4), ND, HEADS * VW], F32, kind="Internal").ap()
        m_scr = nc.dram_tensor("m_scr", [RING, 2, NG, HEADS, 2, P], BF16, kind="Internal").ap()
        g_scr = nc.dram_tensor("g_scr", [batches, 3 * DIM], F32, kind="Internal").ap()

        ident = sb("ident", [P, P])
        iota8 = sb("iota8", [P, NEXP])
        neg_half = sb("neg_half", [P, 2])
        w_hi = sb("w_hi", [P, 5120], F32R)
        w_lo = sb("w_lo", [P, 5120], F32R)
        gatew = sb("gatew", [P, CH, NEXP])
        bqk = sb("bqk", [P, 2, CH])
        bv_bc = sb("bv_bc", [P, DIM])
        modT = sb("modT", [P, 4 * CH * batches + 1])
        onehot = sb("onehot", [P, SLOTS], F32)
        cT = sb("cT", [P, CH, batches])
        sT_c = sb("sT_c", [P, CH, batches])
        gates8 = sb("gates8", [batches, 3 * DIM])

        bo8 = sb("bo8", [batches, DIM])

        QS = sb("QS", [P, RING, HP, CH, 2 * P], BF16)
        KS = sb("KS", [P, RING, HP, CH, 2 * P], BF16)
        KD = sb("KD", [P, HP * CH, SLOTS, ND], BF16)
        v_ring = sb("v_ring", [P, RING, 2 * HEADS * VW + 16])
        v_own = v_ring[:, :, 0:2 * HEADS * VW].rearrange("p u (i h w) -> p u i h w", i=2, h=HEADS)
        own_sb = sb("own_sb", [P, 2, P])
        v_dil = sb("v_dil", [P, 2, HEADS * VW])
        v_blk = sb("v_blk", [P, 2, HEADS, 4, VW])
        probs = sb("probs", [P, PROBS, CH, 2, P])
        mx = sb("mx", [P, 2, HP, CH, 8])
        negm = sb("negm", [P, NG, HEADS])
        mparts = sb("mparts", [P, 2, NG, HEADS], BF16)
        identb = sb("identb", [P, P], BF16)
        mT = sb("mT", [P, 2, P], BF16)
        rsum = sb("rsum", [P, 2, 4 * NG])
        o_grp = sb("o_grp", [P, HEADS, NG, DK])
        o_half = sb("o_half", [P, HEADS, 2, DK])
        o_sum = sb("o_sum", [P, 2, HEADS, DK])

        x_in = sb("x_in", [P, 2, 2, DIM])
        x_res = sb("x_res", [P, 2, 2, DIM])
        gates = sb("gates", [P, 2, 3 * DIM])
        st1 = sb("st1", [P, 2, 6])
        mv1 = sb("mv1", [P, 2, 2])
        ve1 = sb("ve1", [P, 2])
        rs1 = sb("rs1", [P, 2])
        st2 = sb("st2", [P, 2, 6])
        mv2 = sb("mv2", [P, 2, 2])
        ve2 = sb("ve2", [P, 2])
        rs2 = sb("rs2", [P, 2])
        h32 = sb("h32", [P, CH, 2 * P])
        h_hi = sb("h_hi", [P, CH, 2 * P], F32R)
        h_lo = sb("h_lo", [P, CH, 2 * P], F32R)
        qk32 = sb("qk32", [P, 2, CH, 2 * P])
        parts = sb("parts", [P, 2, 3, CH * 2 * P], BF16)

        oT_hi = sb("oT_hi", [P, CH, 2 * P], F32R)
        oT_lo = sb("oT_lo", [P, CH, 2 * P], F32R)
        xn2 = sb("xn2", [P, 2, DIM])
        g32 = sb("g32", [P, CH, 2 * P])
        g_hi = sb("g_hi", [P, CH, 2 * P], F32R)
        g_lo = sb("g_lo", [P, CH, 2 * P], F32R)
        logits = sb("logits", [P, 2, NEXP])
        top = sb("top", [P, 2, NEXP])
        topi = sb("topi", [P, 2, NEXP], U32)
        topf = sb("topf", [P, 2, 2])
        dlt = sb("dlt", [P, 2])
        ed = sb("ed", [P, 2])
        den = sb("den", [P, 2])
        wsel = sb("wsel", [P, 2, 2])
        wone = sb("wone", [P, 2, 2, NEXP])
        wexp = sb("wexp", [P, 2, NEXP])
        th = sb("th", [P, ER])
        s_act = sb("s_act", [P, 2, ER])
        y32 = sb("y32", [P, 2, DIM])
        sT_hi = sb("sT_hi", [P, 2, 4, P], F32R)
        sT_lo = sb("sT_lo", [P, 2, 4, P], F32R)

        gtmp = view(x_res[0:batches, 0, 0, 0:1], [(2 * DIM, 2), (1, 2 * DIM)])
        stage = view(KS[:, 0, 0, 0, 0:2 * P].bitcast(F32), [(1, 8192)])

        ps_m = [ctx.enter_context(nc.psum_tensor(f"ps_m{n}", [P, 512], F32)) for n in range(2)]
        ps_s = [ctx.enter_context(nc.psum_tensor(f"ps_s{n}", [P, 512], F32)) for n in range(2)]
        ps_o = [ctx.enter_context(nc.psum_tensor(f"ps_o{n}", [P, 512], F32)) for n in range(2)]
        ps_d = [ctx.enter_context(nc.psum_tensor(f"ps_d{n}", [P, 512], F32)) for n in range(2)]
        lgts = ps_d[0][:, 0:2 * NEXP]
        maxT = ps_d[0][0:NG * HEADS, 0:P]

        mods_in = sem("mods_in")
        const_in = sem("const_in")
        gates_out = sem("gates_out")
        pads_out = sem("pads_out")
        setup_v = sem("setup_v")
        setup_p = sem("setup_p")
        setup_a = sem("setup_a")
        setup_t = sem("setup_t")
        x_loaded = sem("x_loaded")
        res_loaded = sem("res_loaded")
        part_out = [sem("qpart_out"), sem("kpart_out")]
        stack_in = [sem("q_stacked"), sem("k_stacked")]
        v_out = sem("v_out")
        vdil_in = [sem("vdil_in0"), sem("vdil_in1")]
        m_out = sem("m_out")
        m_in = [sem("m_in0"), sem("m_in1")]
        stored = sem("stored")
        xT_done = sem("xT_done")
        qkv_done = sem("qkv_done")
        mT_done = sem("mT_done")
        oT_done = sem("oT_done")
        attn_done = sem("attn_done")
        gT_done = sem("gT_done")
        lg_done = sem("lg_done")
        uv_done = sem("uv_done")
        sT_done = sem("sT_done")
        down_done = sem("down_done")
        sm_done = sem("sm_done")
        ss_done = sem("ss_done")
        av_done = sem("av_done")
        own_evac = sem("own_evac")
        own_back = sem("own_back")
        ln1_done = sem("ln1_done")
        ln1_var = sem("ln1_var")
        rs1_done = sem("rs1_done")
        h_full = sem("h_full")
        h_evac = sem("h_evac")
        h_split = sem("h_split")
        qk_evac = sem("qk_evac")
        qk_high = sem("qk_high")
        qk_split = sem("qk_split")
        v_evac = sem("v_evac")
        kd_done = sem("kd_done")
        max_done = sem("max_done")
        mp_done = sem("mp_done")
        mT_evac = sem("mT_evac")
        exp_done = sem("exp_done")
        vblk_done = sem("vblk_done")
        norm_done = sem("norm_done")
        osum_done = sem("osum_done")
        oT_evac = sem("oT_evac")
        oT_split = sem("oT_split")
        attn_evac = sem("attn_evac")
        xb_done = sem("xb_done")
        ln2_var = sem("ln2_var")
        rs2_done = sem("rs2_done")
        ln2_done = sem("ln2_done")
        g_full = sem("g_full")
        g_evac = sem("g_evac")
        g_split = sem("g_split")
        lg_read = sem("lg_read")
        dlt_done = sem("dlt_done")
        ed_done = sem("ed_done")
        w_done = sem("w_done")
        th_done = sem("th_done")
        s1_done = sem("s1_done")
        s2_done = sem("s2_done")
        s3_done = sem("s3_done")
        sT_evac = sem("sT_evac")
        sT_split = sem("sT_split")
        y_done = sem("y_done")
        res_done = sem("res_done")
        x1_done = sem("x1_done")
        own_ln1 = sem("own_ln1")
        own_ln2 = sem("own_ln2")
        own_mp = sem("own_mp")
        own_nm = sem("own_nm")
        own_tt = sem("own_tt")
        own_qk = sem("own_qk")
        own_os = sem("own_os")
        settled = sem("settled")

        block = ctx.enter_context(nc.Block())

        def on(pair):
            return not isinstance(pair, int) or 0 <= pair < pairs

        def done(pair):
            return min(max(pair + 1, 0), pairs) if isinstance(pair, int) else pair + 1

        def rows_of(t, pair):
            if isinstance(pair, int):
                return t[pair]
            return t[bass.ds(pair, 1)].rearrange("a p i d -> (a p) i d")

        def run_steps(eng, step):
            for p in range(-4, RING):
                step(p, p % RING)
            with eng.Fori(1, pairs // RING - 1) as it:
                for u in range(RING):
                    step(RING * it + u, u)
            for p in range(pairs - RING, pairs + 2):
                step(p, p % RING)

        def seq_of(pair):
            return pair >> seq_shift

        def v_slot(pair):
            return (pair + 2 * seq_of(pair)) * 2 + 2

        @block.sync
        def _(sp):
            loads = 0

            def const_load(dst, src, loaded=const_in):
                sp.dma_start(dst, src).then_inc(loaded, 16)
                return 1

            def staged(at, n):
                return stage[:, at:at + n]

            with nc.allow_non_contiguous_dma(reason="small constants, once"):
                for k in range(CH):
                    const_load(cT[:, k, :], c[:, k * P:(k + 1) * P].rearrange("b p -> p b"), mods_in)
            const_load(staged(5120, 3072).rearrange("p (k n) -> p k n", k=CH),
                       wmod.rearrange("(k p) n -> p k n", p=P), mods_in)
            with nc.allow_non_contiguous_dma(reason="small constants, once"):
                loads += const_load(bqk[:, 0, :], bq.rearrange("(k p) -> p k", p=P))
                loads += const_load(bqk[:, 1, :], bk.rearrange("(k p) -> p k", p=P))
            loads += const_load(bo8[:, :], bass.AP(bo.tensor, 0, [[0, batches], [1, DIM]]))
            loads += const_load(bv_bc[:, :], bass.AP(bv.tensor, 0, [[0, P], [1, DIM]]))
            loads += const_load(gatew[:, :, :], gate_w.rearrange("(k p) e -> p k e", p=P))
            for n, w in enumerate((wq, wk, wv)):
                loads += const_load(staged(512 * n, 512).rearrange("p (k n) -> p k n", k=CH),
                                    w.rearrange("(k p) n -> p k n", p=P))
            for j in range(HP):
                for k in range(CH):
                    row = (2 * j + k) % HP * DK
                    loads += const_load(stage[row:row + DK, 1536 + (j // 4) * DIM:1536 + (j // 4 + 1) * DIM],
                                        wo[(k * HP + j) * DK:(k * HP + j + 1) * DK, :])
            for n, w in enumerate((w_up, w_gate)):
                for k in range(CH):
                    loads += const_load(
                        staged(2048 + 1024 * n + 512 * k, 512).rearrange("p (e r) -> p e r", e=NEXP),
                        w[:, k * P:(k + 1) * P, :].rearrange("e p r -> p e r"))
            loads += const_load(staged(4096, 1024).rearrange("p (k n) -> p k n", k=4),
                                w_down.rearrange("e r n -> (e r) n").rearrange("(k p) n -> p k n", p=P))
            assert loads == CONST_LOADS
            sp.wait_ge(setup_v, GATES_READY)
            sp.dma_start(g_scr, gates8[:, :]).then_inc(gates_out, 16)
            sp.wait_ge(setup_p, 1)
            for b in range(batches):
                for e in (0, segs + 2):
                    at = b * (segs + 4) + e
                    sp.dma_start(v_scr[at:at + 2, :, :].rearrange("s j w -> (s j) w"),
                                 v_blk[0:2 * ND, 0, 0:4, :, :].rearrange("p a g w -> p (a g w)"),
                                 ).then_inc(pads_out, 16)
            sp.wait_ge(gates_out, 16)
            sp.wait_ge(pads_out, 32 * batches)

            def maxima(pair, u, i):
                wait_apart(sp, mT_evac, 2 * pair + i + 1, settled)
                sp.dma_start(m_scr[u, i].rearrange("g h a q -> (g h) a q"), mT[0:NG * HEADS, :, :]).then_inc(m_out, 16)
                wait_apart(sp, m_out, 16 * (2 * pair + i + 1), settled)
                wait_apart(sp, m_in[i], 32 * pair, settled)
                for a in range(2):
                    row = STACK + a * SLOTS + 2 * u + i
                    sp.dma_start(QS[row:row + NG, u, :, :, i * P:(i + 1) * P].rearrange("g j k q -> g (j k) q"),
                                 m_scr[u, i, :, :, a, :]).then_inc(m_in[i], 16)

            def stacks(pair, u, n):
                wait_apart(sp, part_out[n], 16 * (pair + 1), settled)
                wait_apart(sp, ss_done, 16 * (pair - RING + 1), settled)
                wait_apart(sp, stack_in[n], 96 * pair, settled)
                dst = (QS, KS)[n]
                for blk, part in enumerate((Q_PARTS, K_PARTS)[n]):
                    row = 3 * CH * 2 * P
                    src = bass.AP(part_scr.tensor, part_scr[u, n, 0, part, 0:1].offset,
                                  [[row, DK], [DK * row, HP], [1, CH * 2 * P]])
                    sp.dma_start(dst[blk * DK:(blk + 1) * DK, u, :, :, :].rearrange("c j k t -> c j (k t)"),
                                 src).then_inc(stack_in[n], 16)

            def load_x(p, u):
                wait_apart(sp, x_loaded, 16 * p, settled)
                wait_apart(sp, xT_done, p - 1, settled)
                sp.dma_start(x_in[:, u % 2, :, :], rows_of(x_pairs, p)).then_inc(x_loaded, 16)

            def step(p, u):
                if not isinstance(p, int):
                    load_x(p + 4, u)
                if on(p - 1):
                    wait_apart(sp, res_loaded, 32 * (p - 1), settled)
                    wait_apart(sp, stored, 16 * (p - 2), settled)
                    sp.dma_start(x_res[:, (u + 1) % 2, :, :], rows_of(x_pairs, p - 1)).then_inc(res_loaded, 16)
                    sp.dma_start(gates[:, (u + 1) % 2, :],
                                 bass.AP(g_scr.tensor, seq_of(p - 1) * (3 * DIM), [[0, P], [1, 3 * DIM]])
                                 ).then_inc(res_loaded, 16)
                if on(p):
                    wait_apart(sp, v_out, 16 * done(p + 1), settled)
                    wait_apart(sp, vblk_done, 2 * p, settled)
                    sp.dma_start(v_dil[:, 1, :], neighbours(v_slot(p) + 1)).then_inc(vdil_in[1], 16)
                if on(p + 1):
                    wait_apart(sp, v_out, 16 * done(p + 2), settled)
                    wait_apart(sp, vblk_done, 2 * p + 1, settled)
                    sp.dma_start(v_dil[:, 0, :], neighbours(v_slot(p + 1))).then_inc(vdil_in[0], 16)
                if on(p):
                    maxima(p, u, 1)
                a = (u + 3) % RING
                if on(p + 3):
                    for n in range(2):
                        wait_apart(sp, qk_split, 2 * (p + 3) + n + 1, settled)
                        sp.dma_start(part_scr[a, n].rearrange("p s t -> p (s t)"),
                                     parts[:, n, :, :].rearrange("p s t -> p (s t)")).then_inc(part_out[n], 16)
                        stacks(p + 3, a, n)
                        if n == 0 and isinstance(p, int) and p < RING - 1 and on(p + 5):
                            load_x(p + 5, u + 1)
                if on(p + 1):
                    maxima(p + 1, (u + 1) % RING, 0)
                if on(p - 2):
                    wait_apart(sp, res_done, p - 1, settled)
                    sp.dma_start(rows_of(out_pairs, p - 2), x_res[:, u % 2, :, :]).then_inc(stored, 16)
                if on(p + 3):
                    wait_apart(sp, v_out, 16 * (p + 3), settled)
                    wait_apart(sp, v_evac, p + 4, settled)
                    at = v_slot(p + 3)
                    sp.dma_start(
                        bass.AP(v_scr.tensor, at * vseg_words, [[HEADS * VW, ND], [vseg_words, 2], [1, HEADS * VW]]),
                        v_own[0:P:DIL, a, :, :, :].rearrange("p i h w -> p i (h w)")).then_inc(v_out, 16)

            def neighbours(slot):
                return bass.AP(v_scr.tensor, (slot - 2) * vseg_words,
                               [[3 * vseg_words, 2], [HEADS * VW, 2 * ND], [1, HEADS * VW]])

            load_x(0, 0)
            load_x(1, 1)
            run_steps(sp, step)
            sp.wait_ge(stored, 16 * pairs)
            sp.wait_ge(v_out, 16 * pairs)
            sp.wait_ge(m_out, 32 * pairs)
            for n in range(2):
                sp.wait_ge(part_out[n], 16 * pairs)

        @block.tensor
        def _(pe):
            def split_mm(dst, stat, mov, first, last):
                (s_hi, s_lo), (m_hi, m_lo) = stat, mov
                nc.tensor.matmul(dst, s_hi, m_hi, start=first, stop=False)
                nc.tensor.matmul(dst, s_hi, m_lo, start=False, stop=False)
                return nc.tensor.matmul(dst, s_lo, m_hi, start=False, stop=last)

            def w(at, n):
                return w_hi[:, at:at + n], w_lo[:, at:at + n]

            pe.wait_ge(setup_a, 2)
            pe.wait_ge(mods_in, 16 * MOD_LOADS)
            mods = stage[:, 5120:8192].rearrange("p (k n) -> p k n", k=CH)
            for n, m in enumerate((1, 0, 4, 3)):
                for k in range(CH):
                    at = (n * CH + k) * batches
                    for kk in range(CH):
                        col = m * DIM + k * P
                        nc.tensor.matmul(ps_d[0][:, at:at + batches], mods[:, kk, col:col + P], sT_c[:, kk, :],
                                         start=(kk == 0), stop=(kk == CH - 1))
            for n, m in enumerate((2, 5)):
                for kk in range(CH):
                    mm = nc.tensor.matmul(ps_d[1][0:batches, n * DIM:(n + 1) * DIM], sT_c[:, kk, :],
                                          mods[:, kk, m * DIM:(m + 1) * DIM], start=(kk == 0), stop=(kk == CH - 1))
            mm.then_inc(setup_t, 1)
            pe.wait_ge(const_in, 16 * CONST_LOADS)
            pe.wait_ge(setup_v, WEIGHTS_READY)
            pe.wait_ge(setup_p, SETUP_P)

            def bank_left(p, last, *before):
                wait(pe, *last)
                if isinstance(p, int):
                    for use in before:
                        wait(pe, *use)

            def x_transposed(p, u):
                pe.wait_ge(ln1_done, p + 1)
                bank_left(p, (s2_done, 2 * done(p - 5)), (qk_evac, 2 * done(p - 1)))
                for k in range(CH):
                    for i in range(2):
                        mm = nc.tensor.transpose(ps_d[0][:, (2 * k + i) * P:(2 * k + i + 1) * P],
                                                 x_in[:, u % 2, i, k * P:(k + 1) * P], ident[:, :])
                mm.then_inc(xT_done, 1)

            def down(p, i):
                pe.wait_ge(sT_split, 2 * p + 2)
                if i == 0:
                    bank_left(p, (oT_split, done(p + 1)))
                for e in range(4):
                    mm = split_mm(ps_d[1][:, i * DIM:(i + 1) * DIM], (sT_hi[:, i, e, :], sT_lo[:, i, e, :]),
                                  w(4096 + e * DIM, DIM), e == 0, e == 3)
                if i == 1:
                    mm.then_inc(down_done, 1)

            def maxima_transposed(p, i):
                pe.wait_ge(mp_done, 2 * p + i + 1)

                if i == 1:
                    bank_left(p, (qk_evac, 2 * done(p + 3) - (1 if on(p + 3) else 0)),
                              (s2_done, 2 * done(p - 2)))
                else:
                    bank_left(p, (attn_evac, done(p - 2)), (qk_evac, 2 * done(p + 2)))
                for a in range(2):
                    mm = nc.tensor.transpose(maxT[:, a * 64:(a + 1) * 64].bitcast(BF16),
                                             mparts[:, a, :, :].rearrange("p g h -> p (g h)"), identb[:, :])
                mm.then_inc(mT_done, 1)

            def experts_transposed(p, i):
                pe.wait_ge(s3_done, 2 * p + i + 1)
                if i == 0:
                    pe.wait_ge(s1_done, 2 * p + 2)
                else:
                    pe.wait_ge(sT_split, 2 * p + 1)
                for e in range(4):
                    mm = nc.tensor.transpose(ps_d[1][:, e * P:(e + 1) * P], s_act[:, i, e * P:(e + 1) * P],
                                             ident[:, :])
                mm.then_inc(sT_done, 1)

            def project(p, n):
                pe.wait_ge(h_split, p + 1)
                if n == 1:
                    bank_left(p, (mT_evac, 2 * done(p - 3)), (qk_evac, 2 * p + 1))
                for k in range(CH):
                    for kk in range(CH):
                        mm = split_mm(ps_d[0][:, k * 2 * P:(k + 1) * 2 * P],
                                      w(512 * n + kk * DIM + k * P, P),
                                      (h_hi[:, kk, :], h_lo[:, kk, :]), kk == 0, kk == CH - 1)
                mm.then_inc(qkv_done, 1)

            def project_v(p):
                bank_left(p, (sT_split, 2 * done(p - 5)), (oT_split, done(p - 5)), (v_evac, p))
                for i in range(2):
                    for kk in range(CH):
                        mm = split_mm(ps_d[1][:, i * DIM:(i + 1) * DIM],
                                      (h_hi[:, kk, i * P:(i + 1) * P], h_lo[:, kk, i * P:(i + 1) * P]),
                                      w(1024 + kk * DIM, DIM), kk == 0, kk == CH - 1)
                mm.then_inc(qkv_done, 1)

            def o_transposed(p):
                pe.wait_ge(osum_done, 2 * p + 2)
                bank_left(p, (v_evac, done(p + 4)), (sT_split, 2 * done(p - 1)))
                for k in range(CH):
                    for i in range(2):
                        mm = nc.tensor.transpose(
                            ps_d[1][:, (2 * k + i) * P:(2 * k + i + 1) * P],
                            o_sum[:, i, k * HP:(k + 1) * HP, :].rearrange("p h c -> p (h c)"), ident[:, :])
                mm.then_inc(oT_done, 1)

            def project_out(p):
                pe.wait_ge(oT_split, p + 1)
                bank_left(p, (qk_evac, 2 * done(p + 4)), (mT_evac, 2 * done(p + 1)), (s2_done, 2 * done(p - 1)))
                for i in range(2):
                    for kk in range(CH):
                        mm = split_mm(ps_d[0][:, i * DIM:(i + 1) * DIM],
                                      (oT_hi[:, kk, i * P:(i + 1) * P], oT_lo[:, kk, i * P:(i + 1) * P]),
                                      w(1536 + kk * DIM, DIM), kk == 0, kk == CH - 1)
                mm.then_inc(attn_done, 1)

            def g_transposed(p):
                pe.wait_ge(ln2_done, p + 1)
                pe.wait_ge(mT_evac, min(2 * p + 5, 2 * pairs) if isinstance(p, int) else 2 * p + 5)
                for k in range(CH):
                    for i in range(2):
                        mm = nc.tensor.transpose(ps_d[0][:, (2 * k + i) * P:(2 * k + i + 1) * P],
                                                 xn2[:, i, k * P:(k + 1) * P], ident[:, :])
                mm.then_inc(gT_done, 1)

            def gate_logits(p):
                pe.wait_ge(g_evac, p + 1)
                for i in range(2):
                    for kk in range(CH):
                        mm = nc.tensor.matmul(lgts[:, i * NEXP:(i + 1) * NEXP], g32[:, kk, i * P:(i + 1) * P],
                                              gatew[:, kk, :], start=(kk == 0), stop=(kk == CH - 1))
                mm.then_inc(lg_done, 1)

            def experts_up(p, i, n):
                pe.wait_ge(g_split, p + 1)
                if i == 1:
                    pe.wait_ge((s1_done, s2_done)[n], 2 * p + 1)
                elif n == 0:
                    bank_left(p, (y_done, done(p - 1)), (oT_split, p + 1))
                else:
                    pe.wait_ge(lg_read, p + 1)
                for kk in range(CH):
                    mm = split_mm(ps_d[1 - n][:, :],
                                  (g_hi[:, kk, i * P:(i + 1) * P], g_lo[:, kk, i * P:(i + 1) * P]),
                                  w(2048 + 1024 * n + 512 * kk, ER), kk == 0, kk == CH - 1)
                mm.then_inc(uv_done, 1)

            def near_keys(rows, j, k, r):
                return view(KD[0:rows, 2 * j + k, r, 0:1], [(3 * ND, 2), (1, 2 * ND)])

            def scores_for_max(p, u, t):
                i, j = divmod(t, HP)
                if t == 0 and isinstance(p, int) and p == 0:
                    pe.wait_ge(setup_v, SETUP_V)
                    pe.wait_ge(setup_a, SETUP_A)
                if t == 0:
                    pe.wait_ge(stack_in[0], 96 * (p + 1))
                    pe.wait_ge(stack_in[1], 96 * (p + 1))
                    pe.wait_ge(kd_done, min(2 * p + 3, 2 * pairs) if isinstance(p, int) else 2 * p + 3)
                if t == HP:
                    pe.wait_ge(kd_done, 2 * done(p + 1))
                wait(pe, max_done, 16 * p + t - 1)
                bank = ps_m[t % 2]
                own = slice(i * P, (i + 1) * P)
                for k in range(CH):
                    q = QS[0:STACK, u, j, k, own]
                    nc.tensor.matmul(bank[:, 2 * k * P:(2 * k + 1) * P], q, KS[0:STACK, u, j, k, own],
                                     start=True, stop=True)
                    mm = nc.tensor.matmul(bank[:, (2 * k + 1) * P:(2 * k + 2) * P], q,
                                          near_keys(STACK, j, k, 2 * u + i), start=True, stop=True)
                mm.then_inc(sm_done, 1)

            def scores_for_exp(p, u, t):
                i, j = divmod(t, HP)
                if j == 0:
                    pe.wait_ge(m_in[i], 32 * (p + 1))
                wait(pe, exp_done, 16 * p + t - 1)
                bank = ps_s[t % 2]
                own = slice(i * P, (i + 1) * P)
                for k in range(CH):
                    q = QS[0:ROWS, u, j, k, own]
                    nc.tensor.matmul(bank[:, 2 * k * P:(2 * k + 1) * P], KS[0:ROWS, u, j, k, own], q,
                                     start=True, stop=True)
                    for half in range(2):
                        slot = 2 * u + i + 3 * half
                        mm = nc.tensor.matmul(
                            bank[half * 2 * ND:(half + 1) * 2 * ND, (2 * k + 1) * P:(2 * k + 2) * P],
                            KD[0:ROWS, 2 * j + k, slot:slot + 2, :].rearrange("p s n -> p (s n)"), q,
                            start=True, stop=True)
                mm.then_inc(ss_done, 1)

            def probs_times_v(p, u, t):
                i, j = divmod(t, HP)
                pe.wait_ge(exp_done, 16 * p + t + 1)
                if t == 0:
                    pe.wait_ge(v_evac, p + 1)
                if j == 0:
                    pe.wait_ge(vblk_done, 2 * p + i + 1)
                n = t // 2
                if t % 2 == 0:
                    wait(pe, norm_done, 8 * p + n - 1)
                bank = ps_o[n % 2]
                for k in range(CH):
                    at = (2 * (t % 2) + k) * OW
                    pr = probs[:, t % PROBS, k, :, :]
                    mm = nc.tensor.matmul(bank[:, at:at + 4 * VW], pr[:, 1, :],
                                          v_blk[:, i, k * HP + j, :, :].rearrange("p g w -> p (g w)"),
                                          start=True, stop=True)
                    if n == 7:
                        mm = nc.tensor.matmul(bank[:, at + 4 * VW:at + NG * VW], pr[:, 0, :],
                                              v_own[:, u, i, k * HP + j, :], start=True, stop=True)
                if t % 2 and n < 7:
                    for h in range(4):
                        half, k = divmod(h, CH)
                        v = v_own[:, u, i, k * HP + j - 1 + half, 0:1]
                        mm = nc.tensor.matmul(bank[h * HC:(h + 1) * HC, 512 - P:512], view(v, [(1, HC)]),
                                              probs[:, (t - 1 + half) % PROBS, k, 0, :], start=True, stop=True)
                mm.then_inc(av_done, 1)

            def own_transposed(p, n):
                pe.wait_ge(own_evac, 7 * p + n + 1)
                nc.tensor.transpose(view(ps_o[n % 2][:, 4 * VW:4 * VW + 1], [(OW, 4), (1, HC)]),
                                    own_sb[:, n % 2, :], ident[:, :]).then_inc(own_back, 1)

            def step(p, u):
                for t in range(16):
                    if t in (0, 2) and on(p - 2):
                        experts_transposed(p - 2, t // 2)
                    if t == 1 and on(p + 3):
                        x_transposed(p + 3, (u + 3) % RING)
                    if t == 4 and on(p + 3):
                        project_v(p + 3)
                    if t == 4 and on(p):
                        maxima_transposed(p, 1)
                    if t == 5 and on(p - 1):
                        o_transposed(p - 1)
                    if t == 5 and on(p + 3):
                        project(p + 3, 1)
                    if t == 7 and on(p - 1):
                        project_out(p - 1)
                    if t in (8, 9) and on(p - 2):
                        down(p - 2, t - 8)
                    if t == 10 and on(p - 1):
                        g_transposed(p - 1)
                    if t >= 12 and on(p - 1):
                        experts_up(p - 1, (t - 12) // 2, t % 2)
                    if on(p):
                        scores_for_exp(p, u, t)
                    if on(p + 1):
                        scores_for_max(p + 1, (u + 1) % RING, t)
                    if t == 9 and on(p + 1):
                        maxima_transposed(p + 1, 0)
                    if t >= 2 and on(p):
                        probs_times_v(p, u, t - 2)
                    if t < 2 and on(p - 1):
                        probs_times_v(p - 1, (u + 3) % RING, t + 14)
                    if t == 0 and on(p - 1):
                        own_transposed(p - 1, 6)
                    if t >= 4 and t % 2 == 0 and on(p):
                        own_transposed(p, (t - 4) // 2)
                    if t == 3 and on(p + 3):
                        project(p + 3, 0)

                    if t == 11 and on(p - 1):
                        gate_logits(p - 1)

            run_steps(pe, step)

        @block.scalar
        def _(act):
            act.wait_ge(mods_in, 16 * MOD_LOADS)
            nc.scalar.activation(sT_c[:, :, :], cT[:, :, :], ACT.Tanh, scale=0.5).then_inc(setup_a, 1)
            act.wait_ge(setup_v, SILU_READY)
            nc.scalar.activation(sT_c[:, :, :], sT_c[:, :, :], ACT.Copy, scale=0.5).then_inc(setup_a, 1)
            act.wait_ge(setup_p, SETUP_P)
            for slot in range(SLOTS):
                nc.scalar.activation(KD[STACK:P, :, slot, :],
                                     view(QS[STACK:P, 0, 0, 0, 0:1], [(2 * P, HEADS), (1, ND)]),
                                     ACT.Identity, bias=onehot[STACK:P, slot:slot + 1]).then_inc(setup_a, 1)
            act.wait_ge(setup_v, WEIGHTS_READY)
            for i in range(2):
                slot = 2 * (RING - 1) + i + 2
                nc.scalar.activation(view(KS[STACK:P, RING - 1, 0, 0, i * P:i * P + 1], [(2 * P, HEADS), (1, P)]),
                                     view(QS[STACK:P, RING - 1, 0, 0, i * P:i * P + 1], [(2 * P, HEADS), (1, P)]),
                                     ACT.Identity, bias=onehot[STACK:P, slot:slot + 1]).then_inc(setup_a, 1)

            def mod(n, k, pair):
                return modT[:, bass.ds((n * CH + k) * batches + seq_of(pair), 1)]

            def modulated(p, n, full, high, full_done):
                for k in range(CH):
                    ins = nc.scalar.activation(full[:, k, :], ps_d[0][:, k * 2 * P:(k + 1) * 2 * P],
                                               ACT.Identity, scale=mod(n, k, p), bias=mod(n + 1, k, p))
                ins.then_inc(full_done, 1)
                act.wait_ge(full_done, p + 1)
                return nc.scalar.activation(high[:, :, :].rearrange("p k t -> p (k t)"),
                                            full[:, :, :].rearrange("p k t -> p (k t)"), ACT.Copy)

            def near_copy(p, u, i):
                if i == 0:
                    act.wait_ge(stack_in[1], 96 * (p + 1))
                wait(act, ss_done, 16 * (p - 3) + 8 * i + 8)
                for slot in range((2 * u + i + 2) % 8, SLOTS, 8):
                    src = view(KS[0:STACK, u, 0, 0, i * P:i * P + 1], [(2 * P, HEADS), (DIL, ND)])
                    ins = nc.scalar.activation(KD[0:STACK, :, slot, :], src, ACT.Copy)
                ins.then_inc(kd_done, 1)

            def v_blocks(p, i):
                act.wait_ge(vdil_in[i], 16 * (p + 1))
                wait(act, av_done, 16 * (p - 1) + 8 * i + 8)
                for g in range(4):
                    rows = slice(g * ND, (g + 1) * ND)
                    ins = nc.scalar.activation(
                        v_blk[rows, i, :, g, 0:DK],
                        v_dil[rows, i, :].rearrange("p (h w) -> p h w", h=HEADS)[:, :, 0:DK], ACT.Copy)
                ins.then_inc(vblk_done, 1)

            def exps(p, t):
                act.wait_ge(ss_done, 16 * p + t + 1)
                wait(act, av_done, 16 * p + t - PROBS + (1 if t % 2 else 2))
                nc.scalar.activation(probs[:, t % PROBS, :, :, :].rearrange("p k n q -> p (k n q)"),
                                     ps_s[t % 2][:, :], ACT.Exp).then_inc(exp_done, 1)

            def own_copy(p, n):
                act.wait_ge(av_done, 16 * p + 2 * n + 2)
                wait(act, own_back, 7 * p + n - 1)
                nc.scalar.activation(own_sb[:, n % 2, :], ps_o[n % 2][:, 512 - P:512],
                                     ACT.Copy).then_inc(own_evac, 1)

            def max_evac(p, i):
                act.wait_ge(mT_done, 2 * p + i + 1)
                wait(act, m_out, 16 * (2 * p + i))
                nc.scalar.activation(mT[0:NG * HEADS, :, :].rearrange("p a q -> p (a q)"),
                                     maxT.bitcast(BF16), ACT.Copy).then_inc(mT_evac, 1)

            def qk_copy(p, n):
                act.wait_ge(qkv_done, 3 * p + 2 * n + 1)
                wait(act, qk_split, 2 * (p - 1) + n + 1)
                for k in range(CH):
                    ins = nc.scalar.activation(qk32[:, n, k, :], ps_d[0][:, k * 2 * P:(k + 1) * 2 * P], ACT.Identity,
                                               scale=(0.25, 1.0)[n], bias=bqk[:, n, k:k + 1])
                ins.then_inc(qk_evac, 1)

            def high_copy(p, n):
                act.wait_ge(qk_evac, 2 * p + n + 1)
                wait(act, part_out[n], 16 * p)
                nc.scalar.activation(parts[:, n, 0, :], qk32[:, n, :, :].rearrange("p k t -> p (k t)"),
                                     ACT.Copy).then_inc(qk_high, 1)

            def s_copy(p, i):
                act.wait_ge(sT_done, 2 * p + i + 1)
                wait(act, down_done, p)
                nc.scalar.activation(sT_hi[:, i, :, :].rearrange("p e t -> p (e t)"), ps_d[1][:, :],
                                     ACT.Copy).then_inc(sT_evac, 1)

            def tanh_u(p, i):
                act.wait_ge(uv_done, 4 * p + 2 * i + 1)
                wait(act, s1_done, 2 * p + i)
                nc.scalar.activation(th[:, :], ps_d[1][:, :], ACT.Tanh, scale=0.5).then_inc(th_done, 1)

            def step(p, u):
                for t in range(16):

                    if t == 0 and on(p - 1):
                        own_copy(p - 1, 6)
                    if t >= 4 and t % 2 == 0 and on(p):
                        own_copy(p, (t - 4) // 2)
                    if t == 4 and on(p):
                        max_evac(p, 1)
                    if t == 4 and on(p + 3):
                        high_copy(p + 3, 0)
                    if t in (0, 2) and on(p - 2):
                        s_copy(p - 2, t // 2)

                    if t == 1 and on(p + 3):
                        act.wait_ge(xT_done, p + 4)
                        wait(act, qkv_done, 3 * (p + 3))
                        modulated(p + 3, 0, h32, h_hi, h_full).then_inc(h_evac, 1)
                    if t == 5 and on(p - 1):
                        act.wait_ge(oT_done, p)
                        wait(act, attn_done, p - 1)
                        nc.scalar.activation(oT_hi[:, :, :].rearrange("p k t -> p (k t)"), ps_d[1][:, :],
                                             ACT.Copy).then_inc(oT_evac, 1)

                    if t == 5 and on(p + 3):
                        qk_copy(p + 3, 1)
                    if t == 9 and on(p + 1):
                        max_evac(p + 1, 0)
                    if t == 10 and on(p - 1):
                        act.wait_ge(gT_done, p)
                        wait(act, uv_done, 4 * (p - 1))
                        modulated(p - 1, 2, g32, g_hi, g_full).then_inc(g_evac, 1)
                    if t in (12, 14) and on(p - 1):
                        tanh_u(p - 1, (t - 12) // 2)
                    if t == 13 and on(p - 1):
                        act.wait_ge(dlt_done, p)
                        nc.scalar.activation(ed[:, :], dlt[:, :], ACT.Exp).then_inc(ed_done, 1)
                    if on(p):
                        exps(p, t)

                    if t == 3 and on(p + 3):
                        qk_copy(p + 3, 0)

                    if t == 7 and on(p + 2):
                        if isinstance(p, int) and p == -2:
                            near_copy(0, 0, 0)
                        near_copy(p + 2, (u + 2) % RING, 1)
                    if t == 6 and on(p + 3):
                        high_copy(p + 3, 1)
                    if t == 6 and on(p):
                        v_blocks(p, 1)
                    if t == 11 and on(p + 1):
                        v_blocks(p + 1, 0)
                    if t == 14 and on(p + 3) and not (isinstance(p, int) and p == -3):
                        near_copy(p + 3, (u + 3) % RING, 0)

            run_steps(act, step)

        @block.vector
        def _(dve):
            setup = [0]

            def setup_inc(ins):
                ins.then_inc(setup_v, 1)
                setup[0] += 1
                dve.wait_ge(setup_v, setup[0])

            setup_inc(nc.vector.memset(v_own[:, :, :, :, DK:VW], 1.0))
            setup_inc(nc.vector.memset(v_ring[:, :, 2 * HEADS * VW:2 * HEADS * VW + 16], 0.0))
            dve.wait_ge(setup_a, 1)
            setup_inc(nc.vector.scalar_tensor_tensor(out=sT_c[:, :, :], in0=sT_c[:, :, :], scalar=1.0,
                                                     in1=cT[:, :, :], op0=ALU.add, op1=ALU.mult))
            assert setup[0] == SILU_READY
            dve.wait_ge(setup_t, 1)
            half = CH * batches
            for n in range(4):
                setup_inc(nc.vector.tensor_scalar(modT[:, n * half:(n + 1) * half],
                                                  ps_d[0][:, n * half:(n + 1) * half],
                                                  1.0 if n % 2 == 0 else 0.0, None, ALU.add))
            raw = gates8[:, 0:2 * DIM]
            setup_inc(nc.vector.tensor_copy(raw, ps_d[1][0:batches, :]))
            setup_inc(nc.vector.tensor_scalar(gtmp[:, 0, :], raw, 0.25, None, ALU.max))
            setup_inc(nc.vector.scalar_tensor_tensor(out=gtmp[:, 0, :], in0=raw, scalar=0.0, in1=gtmp[:, 0, :],
                                                     op0=ALU.is_ge, op1=ALU.mult))
            setup_inc(nc.vector.tensor_scalar(gtmp[:, 1, :], raw, -0.25, None, ALU.min))
            setup_inc(nc.vector.scalar_tensor_tensor(out=gtmp[:, 1, :], in0=raw, scalar=0.0, in1=gtmp[:, 1, :],
                                                     op0=ALU.is_lt, op1=ALU.mult))
            setup_inc(nc.vector.tensor_tensor(raw, gtmp[:, 0, :], gtmp[:, 1, :], ALU.add))
            dve.wait_ge(const_in, 16 * CONST_LOADS)
            setup_inc(nc.vector.tensor_tensor(gates8[:, 2 * DIM:3 * DIM], gates8[:, 0:DIM], bo8[:, :], ALU.mult))
            assert setup[0] == GATES_READY
            setup_inc(nc.vector.tensor_copy(w_hi[:, :], stage[:, 0:5120]))
            setup_inc(nc.vector.tensor_tensor(w_lo[:, :], stage[:, 0:5120], w_hi[:, :].bitcast(F32), ALU.subtract))
            setup_inc(nc.vector.tensor_scalar(bqk[:, 0, :], bqk[:, 0, :], 0.25, None, ALU.mult))
            assert setup[0] == WEIGHTS_READY
            dve.wait_ge(setup_p, SETUP_P)

            def ones():
                for u in range(RING - 1):
                    for i in range(2):
                        slot = 2 * u + i + 2
                        setup_inc(nc.vector.tensor_scalar(
                            view(KS[STACK:P, u, 0, 0, i * P:i * P + 1], [(2 * P, HEADS), (1, P)]),
                            view(QS[STACK:P, u, 0, 0, i * P:i * P + 1], [(2 * P, HEADS), (1, P)]),
                            onehot[STACK:P, slot:slot + 1], None, ALU.add))
                dve.wait_ge(pads_out, 32 * batches)
                for g in range(4):
                    setup_inc(nc.vector.memset(v_blk[g * ND:(g + 1) * ND, :, :, g, DK:VW], 4.0))
                assert setup[0] == SETUP_V, setup[0]

            def layer_norm_stats(src, st, mv, ve, free_sem, free_val, own, at, done):
                for i in range(2):
                    nc.vector.bn_stats(st[:, i, :], src(i)).then_inc(own, 1)
                wait_apart(dve, own, at + 2, settled)
                for i in range(2):
                    nc.vector.bn_aggr(mv[:, i, :], st[:, i, :]).then_inc(own, 1)
                dve.wait_ge(own, at + 4)
                wait(dve, free_sem, free_val)
                nc.vector.tensor_scalar(ve[:, :], mv[:, :, 1], EPS, None, ALU.add).then_inc(done, 1)

            def norm1_stats(p, u):
                dve.wait_ge(x_loaded, 16 * (p + 1))
                layer_norm_stats(lambda i: x_in[:, u % 2, i, :], st1, mv1, ve1, rs1_done, p, own_ln1, 4 * p, ln1_var)

            def norm1(p, u):
                dve.wait_ge(rs1_done, p + 1)
                for i in range(2):
                    ins = nc.vector.tensor_scalar(x_in[:, u % 2, i, :], x_in[:, u % 2, i, :], mv1[:, i, 0:1],
                                                  rs1[:, i:i + 1], ALU.subtract, ALU.mult)
                ins.then_inc(ln1_done, 1)

            def max_parts(p, i):
                dve.wait_ge(max_done, 16 * p + 8 * i + 8)
                wait(dve, mT_done, 2 * p + i)
                m = view(mx[:, i, 0, 0, 0:1], [(8, HEADS), (1, 8)])
                nc.vector.tensor_reduce(negm[:, 2, :], m[:, :, 0:4], AX_X, ALU.max, negate=True)
                for g, at in ((0, 4), (3, 6)):
                    ins = nc.vector.tensor_scalar(negm[:, g:g + 2, :].rearrange("p g h -> p h g"),
                                                  m[:, :, at:at + 2], -1.0, None, ALU.mult)
                ins.then_inc(own_mp, 1)
                dve.wait_ge(own_mp, 2 * (2 * p + i) + 1)
                flat = negm[:, :, :].rearrange("p g h -> p (g h)")
                nc.vector.tensor_copy(mparts[:, 0, :, :].rearrange("p g h -> p (g h)"), flat).then_inc(own_mp, 1)
                dve.wait_ge(own_mp, 2 * (2 * p + i) + 2)
                nc.vector.tensor_tensor(mparts[:, 1, :, :].rearrange("p g h -> p (g h)"), flat,
                                        mparts[:, 0, :, :].rearrange("p g h -> p (g h)"),
                                        ALU.subtract).then_inc(mp_done, 1)

            def maxima(p, t):
                i, j = divmod(t, HP)
                dve.wait_ge(sm_done, 16 * p + t + 1)
                if j == 0:
                    wait(dve, mp_done, 2 * p + i - 1)
                nc.vector.tensor_reduce(mx[:, i, j, :, :].rearrange("p k s -> p (k s)"),
                                        ps_m[t % 2][:, :].rearrange("p (s n) -> p s n", n=ND),
                                        AX_X, ALU.max).then_inc(max_done, 1)

            def normalise(p, n):
                if n < 7:
                    dve.wait_ge(own_back, 7 * p + n + 1)
                else:
                    dve.wait_ge(av_done, 16 * p + 2 * n + 2)
                i, jj = divmod(n, 4)
                if jj == 0:
                    wait(dve, osum_done, 2 * p + i)
                bank = ps_o[n % 2]
                r = rsum[:, n % 2, :]
                nc.vector.reciprocal(r.rearrange("p (h g) -> p h g", h=4),
                                     view(bank[:, DK:DK + 1], [(OW, 4), (VW, NG)])).then_inc(own_nm, 1)
                dve.wait_ge(own_nm, 8 * p + n + 1)
                nc.vector.tensor_tensor(o_grp[:, 4 * jj:4 * jj + 4, :, :],
                                        view(bank[:, 0:1], [(OW, 4), (VW, NG), (1, DK)]),
                                        view(r, [(NG, 4), (1, NG), (0, DK)]), ALU.mult).then_inc(norm_done, 1)

            def v_copy(p, u):
                dve.wait_ge(qkv_done, 3 * p + 2)
                wait(dve, av_done, 16 * (p - 3))
                nc.vector.tensor_tensor(v_own[:, u, :, :, 0:DK],
                                        ps_d[1][:, :].rearrange("p (i h c) -> p i h c", i=2, h=HEADS),
                                        view(bv_bc[:, 0:1], [(0, 2), (DK, HEADS), (1, DK)]),
                                        ALU.add).then_inc(v_evac, 1)

            def attn_out(p, u):
                dve.wait_ge(attn_done, p + 1)
                wait(dve, gT_done, p)
                dve.wait_ge(xb_done, p + 1)
                g = gates[:, u % 2, 0:DIM]
                nc.vector.tensor_tensor(xn2[:, :, :], ps_d[0][:, :].rearrange("p (i d) -> p i d", i=2),
                                        view(g, [(0, 2), (1, DIM)]), ALU.mult).then_inc(attn_evac, 1)
                dve.wait_ge(attn_evac, p + 1)
                nc.vector.tensor_tensor(x_res[:, u % 2, :, :], x_res[:, u % 2, :, :], xn2[:, :, :],
                                        ALU.add).then_inc(x1_done, 1)

            def norm2_stats(p, u):
                dve.wait_ge(x1_done, p + 1)
                layer_norm_stats(lambda i: x_res[:, u % 2, i, :], st2, mv2, ve2, rs2_done, p, own_ln2, 4 * p, ln2_var)

            def norm2(p, u):
                dve.wait_ge(rs2_done, p + 1)
                for i in range(2):
                    ins = nc.vector.tensor_scalar(xn2[:, i, :], x_res[:, u % 2, i, :], mv2[:, i, 0:1],
                                                  rs2[:, i:i + 1], ALU.subtract, ALU.mult)
                ins.then_inc(ln2_done, 1)

            def top_two(p):
                dve.wait_ge(lg_done, p + 1)
                nc.vector.tensor_copy(logits[:, :, :].rearrange("p i e -> p (i e)"),
                                      lgts).then_inc(lg_read, 1)
                wait_apart(dve, lg_read, p + 1, settled)
                for i in range(2):
                    nc.vector.max(top[:, i, :], logits[:, i, :]).then_inc(own_tt, 1)
                dve.wait_ge(own_tt, 9 * p + 2)
                nc.vector.tensor_tensor(dlt[:, :], top[:, :, 1], top[:, :, 0], ALU.subtract).then_inc(dlt_done, 1)
                for i in range(2):
                    nc.vector.max_index(topi[:, i, :], top[:, i, :], logits[:, i, :]).then_inc(own_tt, 1)
                dve.wait_ge(own_tt, 9 * p + 4)
                nc.vector.tensor_copy(topf[:, :, :], topi[:, :, 0:2]).then_inc(own_tt, 1)

            def expert_weights(p):
                dve.wait_ge(ed_done, p + 1)
                nc.vector.tensor_scalar(den[:, :], ed[:, :], 2.0, 2.0, ALU.mult, ALU.add).then_inc(own_tt, 1)
                dve.wait_ge(own_tt, 9 * p + 6)
                nc.vector.reciprocal(wsel[:, 0, :], den[:, :]).then_inc(own_tt, 1)
                dve.wait_ge(own_tt, 9 * p + 7)
                nc.vector.tensor_tensor(wsel[:, 1, :], wsel[:, 0, :], ed[:, :], ALU.mult).then_inc(own_tt, 1)
                dve.wait_ge(own_tt, 9 * p + 8)
                for i in range(2):
                    for n in range(2):
                        ins = nc.vector.tensor_scalar(wone[:, n, i, :], iota8[:, :], topf[:, i, n:n + 1],
                                                      wsel[:, n, i:i + 1], ALU.is_equal, ALU.mult)
                ins.then_inc(own_tt, 1)
                dve.wait_ge(own_tt, 9 * p + 9)
                wait(dve, s3_done, 2 * p)
                nc.vector.tensor_tensor(wexp[:, :, :], wone[:, 0, :, :], wone[:, 1, :, :], ALU.add).then_inc(w_done, 1)

            def gated_u(p, i):
                dve.wait_ge(th_done, 2 * p + i + 1)
                wait(dve, sT_done, 2 * (p - 1) + i + 1)
                nc.vector.scalar_tensor_tensor(out=s_act[:, i, :], in0=th[:, :], scalar=1.0, in1=ps_d[1][:, :],
                                               op0=ALU.add, op1=ALU.mult).then_inc(s1_done, 1)

            def gated_v(p, i):
                dve.wait_ge(s1_done, 2 * p + i + 1)
                dve.wait_ge(uv_done, 4 * p + 2 * i + 2)
                nc.vector.tensor_tensor(s_act[:, i, :], s_act[:, i, :], ps_d[0][:, :], ALU.mult).then_inc(s2_done, 1)

            def experts_out(p, u):
                dve.wait_ge(down_done, p + 1)
                wait(dve, res_done, p)
                nc.vector.tensor_tensor(y32[:, :, :], ps_d[1][:, :].rearrange("p (i d) -> p i d", i=2),
                                        view(gates[:, u % 2, DIM:DIM + 1], [(0, 2), (1, DIM)]),
                                        ALU.mult).then_inc(y_done, 1)

            def low_part(dst, full, high, done):
                nc.vector.tensor_tensor(dst, full, high.bitcast(F32), ALU.subtract).then_inc(done, 1)

            def flat(t):
                return t.rearrange("p k t -> p (k t)")

            def s_low(p, i):
                dve.wait_ge(sT_evac, 2 * p + i + 1)
                low_part(flat(sT_lo[:, i, :, :]), ps_d[1][:, :], flat(sT_hi[:, i, :, :]), sT_split)

            def step(p, u):
                for t in range(16):
                    if t == 0 and on(p - 2):
                        gated_v(p - 2, 1)
                    if t == 0 and on(p):
                        max_parts(p, 1)
                    if t in (0, 2) and on(p - 2):
                        s_low(p - 2, t // 2)
                    if t == 1 and on(p - 1):
                        normalise(p - 1, 6)
                    if t == 3 and on(p + 4) and not (isinstance(p, int) and p == -4):
                        norm1_stats(p + 4, u)
                    if t == 5 and on(p - 1):
                        dve.wait_ge(oT_evac, p)
                        low_part(flat(oT_lo[:, :, :]), ps_d[1][:, :], flat(oT_hi[:, :, :]), oT_split)
                    if t == 6 and on(p + 4) and not (isinstance(p, int) and p == -4):
                        norm1(p + 4, u)
                    if t == 7 and on(p - 1):
                        attn_out(p - 1, u + 1)

                    if t == 8 and on(p - 1):
                        norm2_stats(p - 1, u + 1)
                    if t == 8 and on(p + 1):
                        max_parts(p + 1, 0)
                    if t == 9 and on(p - 1):
                        norm2(p - 1, u + 1)
                    if t == 10 and on(p - 2):
                        experts_out(p - 2, u)
                    if t == 11 and on(p - 1):
                        dve.wait_ge(g_evac, p)
                        low_part(flat(g_lo[:, :, :]), flat(g32[:, :, :]), flat(g_hi[:, :, :]), g_split)

                    if t == 12 and on(p - 1):
                        top_two(p - 1)
                    if t in (13, 15) and on(p - 1):
                        gated_u(p - 1, (t - 13) // 2)
                    if t == 14 and on(p - 1):
                        gated_v(p - 1, 0)
                        expert_weights(p - 1)
                    if t == 4 and on(p + 3):
                        v_copy(p + 3, (u + 3) % RING)
                    if t >= 5 and t % 2 and on(p):
                        normalise(p, (t - 5) // 2)
                    if on(p + 1):
                        maxima(p + 1, t)
                    if t == 1 and on(p - 1):
                        normalise(p - 1, 7)

            norm1_stats(0, 0)
            norm1(0, 0)
            ones()
            run_steps(dve, step)

        @block.gpsimd
        def _(pool):
            nc.gpsimd.memset(v_blk[:, :, :, :, :], 0.0).then_inc(setup_p, 1)
            nc.gpsimd.memset(onehot[:, :], 0.0).then_inc(setup_p, 1)
            nc.gpsimd.memset(ident[:, :], 0.0).then_inc(setup_p, 1)
            nc.gpsimd.memset(identb[:, :], 0.0).then_inc(setup_p, 1)
            nc.gpsimd.memset(neg_half[:, :], -0.5).then_inc(setup_p, 1)
            pool.wait_ge(setup_p, 5)
            count = 5
            for a in range(2):
                nc.gpsimd.affine_select(out=onehot[STACK:P, :], in_=onehot[STACK:P, :], compare_op=ALU.not_equal,
                                        fill=1.0, base=-a * SLOTS, pattern=[[-1, SLOTS]],
                                        channel_multiplier=1).then_inc(setup_p, 1)
                count += 1
                pool.wait_ge(setup_p, count)
            assert count == ONEHOT_READY
            for m in (ident, identb):
                nc.gpsimd.affine_select(out=m[:, :], in_=m[:, :], compare_op=ALU.not_equal, fill=1.0, base=0,
                                        pattern=[[-1, P]], channel_multiplier=1).then_inc(setup_p, 1)
            nc.gpsimd.iota(iota8[:, :], pattern=[[1, NEXP]], base=0, channel_multiplier=0,
                           allow_small_or_imprecise_dtypes=True).then_inc(setup_p, 1)

            nc.gpsimd.memset(view(QS[:, 0, 0, 0, 0:2 * P].bitcast(F32), [(1, 8192)]), 0.0).then_inc(setup_p, 1)
            nc.gpsimd.memset(view(KD[:, 0, 0, 0:2].bitcast(F32), [(1, HEADS * SLOTS * ND // 2)]),
                             0.0).then_inc(setup_p, 1)
            pool.wait_ge(setup_p, SETUP_P)

            def qk_parts(p, n):
                pool.wait_ge(qk_high, 2 * p + n + 1)
                x32 = qk32[:, n, :, :].rearrange("p k t -> p (k t)")
                high, mid, low = (parts[:, n, s, :] for s in range(3))
                at = 2 * (2 * p + n)
                nc.gpsimd.tensor_tensor(x32, x32, high, ALU.subtract).then_inc(own_qk, 1)
                wait_apart(pool, own_qk, at + 1, settled)
                nc.gpsimd.tensor_scalar(mid, x32, 1.0, 0.0, ALU.mult, ALU.add).then_inc(own_qk, 1)
                pool.wait_ge(own_qk, at + 2)
                nc.gpsimd.tensor_tensor(low, x32, mid, ALU.subtract).then_inc(qk_split, 1)

            def sum_groups(p, i):
                pool.wait_ge(norm_done, 8 * p + 4 * i + 4)
                wait(pool, oT_done, p)
                at = 2 * (2 * p + i)
                o = o_grp
                nc.gpsimd.tensor_tensor(o_half[:, :, :, :], o[:, :, 0:2, :], o[:, :, 2:4, :],
                                        ALU.add).then_inc(own_os, 1)
                pool.wait_ge(own_os, at + 1)
                nc.gpsimd.tensor_tensor(o_sum[:, i, :, :], o_half[:, :, 0, :], o_half[:, :, 1, :],
                                        ALU.add).then_inc(own_os, 1)
                pool.wait_ge(own_os, at + 2)
                nc.gpsimd.tensor_tensor(o_sum[:, i, :, :], o_sum[:, i, :, :], o[:, :, 4, :],
                                        ALU.add).then_inc(osum_done, 1)

            def flat(t):
                return t[:, :, :].rearrange("p k t -> p (k t)")

            def expert_weight(p, i):
                pool.wait_ge(s2_done, 2 * p + i + 1)
                pool.wait_ge(w_done, p + 1)
                nc.gpsimd.tensor_tensor(s_act[:, i, :].rearrange("p (e r) -> p e r", e=NEXP),
                                        s_act[:, i, :].rearrange("p (e r) -> p e r", e=NEXP),
                                        view(wexp[:, i, 0:1], [(1, NEXP), (0, RANK)]),
                                        ALU.mult).then_inc(s3_done, 1)

            def last_sum(p, u):
                pool.wait_ge(y_done, p + 1)
                nc.gpsimd.tensor_tensor(x_res[:, u % 2, :, :], x_res[:, u % 2, :, :], y32[:, :, :],
                                        ALU.add).then_inc(res_done, 1)

            def inv_std(ve, rs, var, p, done):
                pool.wait_ge(var, p + 1)
                nc.gpsimd.tensor_tensor(rs[:, :], ve[:, :], neg_half[:, :], ALU.pow).then_inc(done, 1)

            def step(p, u):
                for t in range(16):
                    if t == 0 and on(p - 2):
                        expert_weight(p - 2, 1)
                    if t == 1 and on(p + 3):
                        pool.wait_ge(h_evac, p + 4)
                        wait(pool, qkv_done, 3 * (p + 3))
                        nc.gpsimd.tensor_tensor(flat(h_lo), flat(h32), flat(h_hi).bitcast(F32),
                                                ALU.subtract).then_inc(h_split, 1)
                    if t == 2 and on(p - 1):
                        sum_groups(p - 1, 1)
                    if t == 3 and on(p - 1):
                        pool.wait_ge(res_loaded, 32 * p)
                        r = (u + 1) % 2
                        nc.gpsimd.tensor_tensor(x_res[:, r, :, :], x_res[:, r, :, :],
                                                view(gates[:, r, 2 * DIM:2 * DIM + 1], [(0, 2), (1, DIM)]),
                                                ALU.add).then_inc(xb_done, 1)
                    if t == 4 and on(p + 4):
                        inv_std(ve1, rs1, ln1_var, p + 4, rs1_done)
                    if t in (4, 6) and on(p + 3):
                        qk_parts(p + 3, (t - 4) // 2)
                    if t == 8 and on(p - 1):
                        inv_std(ve2, rs2, ln2_var, p - 1, rs2_done)
                    if t == 10 and on(p - 2):
                        last_sum(p - 2, u)
                    if t == 12 and on(p):
                        sum_groups(p, 0)
                    if t == 14 and on(p - 1):
                        expert_weight(p - 1, 0)

            run_steps(pool, step)



_INS = ["L0_attn_x", "L0_attn_Wq", "L0_attn_bq", "L0_attn_Wk", "L0_attn_bk", "L0_attn_Wv", "L0_attn_bv",
        "L0_attn_Wo", "L0_attn_bo", "L0_ffn_gate_w", "L0_ffn_Wu", "L0_ffn_Wv", "L0_ffn_Wo", "L0_c", "L0_wmod"]
_OUTS = [((8, 2048, 256), "float32")]


def kernel(**inputs):
    import numpy as _np
    import concourse.bacc as _bacc
    from concourse import mybir as _mybir
    from concourse.bass_utils import run_bass_kernel_spmd as _run

    nc = _bacc.Bacc("TRN2", target_bir_lowering=False, num_devices=1, dynamic_dma_scratch_size=1024)
    arrays, args = {}, []
    for name in _INS:
        a = _np.ascontiguousarray(inputs[name])
        arrays[f"in_{name}_dram"] = a
        args.append(nc.dram_tensor(f"in_{name}_dram", a.shape, _mybir.dt.from_np(a.dtype), kind="ExternalInput").ap())
    for i, (shape, dtype) in enumerate(_OUTS):
        dt = _mybir.dt.from_np(_np.dtype(dtype))
        args.append(nc.dram_tensor(f"out_{i}_dram", shape, dt, kind="ExternalOutput").ap())
    adaln_block(nc, *args)
    r = _run(nc, [arrays], core_ids=[0])
    got = tuple(r.results[0][f"out_{i}_dram"] for i in range(len(_OUTS)))
    return got[0]
```
